# Optimizing a Trainium2 kernel written in Bass

```python
import numpy as np
import jax
import jax.numpy as jnp

def _softmax(x, axis=-1):
    return jax.nn.softmax(x, axis=axis)

def _gelu(x):
    return jax.nn.gelu(x, approximate=True)

def _silu(x):
    return jax.nn.silu(x)

def _sigmoid(x):
    return jax.nn.sigmoid(x)

def _layernorm(x, axis=-1, eps=1e-05):
    m = jnp.mean(x, axis=axis, keepdims=True)
    v = jnp.var(x, axis=axis, keepdims=True)
    return (x - m) / jnp.sqrt(v + eps)

def _scatter_add(tgt, idx, src, axis=0):
    return tgt.at[idx].add(src)

def _segment_sum(src, seg, n):
    return jax.ops.segment_sum(src, seg, n)
kernel_name = 'mk_xattn_ffn_d2_seqx_r8_82fb75'

def setup_inputs(seed: int=0):
    np.random.seed(seed)
    _w = jnp.asarray

    def _rec_inputs():
        import jax
        import jax.numpy as jnp
        _rk = jax.random.key(seed)
        x = -0.0002928 + 1 * jax.random.normal(jax.random.fold_in(_rk, 1), (16, 256, 128), jnp.float32)
        _lenS = 256 - jax.random.randint(jax.random.fold_in(_rk, 7), (16,), 0, max(1, 256 // 4) + 1, jnp.int32)
        _lenS2 = 1601 - jax.random.randint(jax.random.fold_in(_rk, 8), (16,), 0, max(1, 1601 // 4) + 1, jnp.int32)
        _ctx_512P = jax.random.normal(jax.random.fold_in(_rk, 11), (16, 16, 64), jnp.float32)
        _ctx_512c = jax.random.dirichlet(jax.random.fold_in(_rk, 511), 0.3 * jnp.ones((16,), jnp.float32), (16, 1601))
        _ctx_512t = jnp.einsum('bsk,bkd->bsd', _ctx_512c, _ctx_512P)
        _ctx_512t = _ctx_512t * jax.lax.rsqrt(jnp.mean(jnp.square(_ctx_512t)) + 1e-12) * 0.953939
        ctx_512 = 0.00222621 + 0.99962 * (_ctx_512t + 0.3 * jax.random.normal(jax.random.fold_in(_rk, 611), (16, 1601, 64), jnp.float32))
        return (x, ctx_512)
    x, ctx_512 = _rec_inputs()

    def _L0_xattn_setup():
        import jax, jax.numpy as jnp
        import numpy as np
        B, T, TC, C, CC, H = (2, 256, 64, 128, 64, 16)
        D = C // H

        def _heads(t):
            b, l, _ = t.shape
            return t.reshape(b, l, H, D).transpose(0, 2, 1, 3)
        key = jax.random.key(seed)
        ks = jax.random.split(key, 18)
        w = lambda k, i, o: jax.random.normal(k, (i, o), jnp.float32) / np.sqrt(i).astype(np.float32)
        return {'x': jax.random.normal(ks[0], (B, T, C), jnp.float32), 'cross_input': jax.random.normal(ks[1], (B, TC, CC), jnp.float32), 'Wk': w(ks[2], C, C), 'bk': jnp.zeros((C,), jnp.float32), 'Wq': w(ks[3], C, C), 'bq': jnp.zeros((C,), jnp.float32), 'Wv': w(ks[4], C, C), 'bv': jnp.zeros((C,), jnp.float32), 'Wck': w(ks[5], CC, C), 'bck': jnp.zeros((C,), jnp.float32), 'Wcq': w(ks[6], C, C), 'bcq': jnp.zeros((C,), jnp.float32), 'Wcv': w(ks[7], CC, C), 'bcv': jnp.zeros((C,), jnp.float32), 'Wp': w(ks[8], C, C), 'bp': jnp.zeros((C,), jnp.float32)}
    _L0_xattn_all = _L0_xattn_setup()
    _L0_xattn_in = {k: v for k, v in _L0_xattn_all.items() if k in ('Wk', 'bk', 'Wq', 'bq', 'Wv', 'bv', 'Wck', 'bck', 'Wcq', 'bcq', 'Wcv', 'bcv', 'Wp', 'bp')}
    del _L0_xattn_all

    def _L0_ffn_setup():
        import jax, jax.numpy as jnp
        import numpy as np
        B, S, D, F, E, K = (4, 256, 128, 512, 8, 2)
        key = jax.random.key(seed)
        ks = jax.random.split(key, 8)
        x = jax.random.normal(ks[0], (B, S, D), dtype=jnp.float32)
        router_w = jax.random.normal(ks[1], (E, D), dtype=jnp.float32) * 0.02
        w1_w = jax.random.normal(ks[2], (E, F, D), dtype=jnp.float32) * 0.02
        w1_b = jax.random.normal(ks[3], (E, F), dtype=jnp.float32) * 0.02
        w2_w = jax.random.normal(ks[4], (E, D, F), dtype=jnp.float32) * 0.02
        w2_b = jax.random.normal(ks[5], (E, D), dtype=jnp.float32) * 0.02
        wg_w = jax.random.normal(ks[6], (E, F, D), dtype=jnp.float32) * 0.02
        wg_b = jax.random.normal(ks[7], (E, F), dtype=jnp.float32) * 0.02
        return {'x': x, 'router_w': router_w, 'w1_w': w1_w, 'w1_b': w1_b, 'w2_w': w2_w, 'w2_b': w2_b, 'wg_w': wg_w, 'wg_b': wg_b}
    _L0_ffn_all = _L0_ffn_setup()
    _L0_ffn_in = {k: v for k, v in _L0_ffn_all.items() if k in ('router_w', 'w1_w', 'w1_b', 'w2_w', 'w2_b', 'wg_w', 'wg_b')}
    del _L0_ffn_all

    def _L1_xattn_setup():
        import jax, jax.numpy as jnp
        import numpy as np
        HEADS = 16
        D_MODEL = 128
        IMG_MODEL = 64
        D_K = D_MODEL // HEADS
        key = jax.random.key(seed)
        ks = jax.random.split(key, 12)
        B, LQ, LKV = (8, 256, 128)
        s_dm = 1.0 / np.sqrt(D_MODEL)
        s_im = 1.0 / np.sqrt(IMG_MODEL)
        return {'q': jax.random.normal(ks[0], (B, LQ, D_MODEL), jnp.float32), 'k': jax.random.normal(ks[1], (B, LKV, IMG_MODEL), jnp.float32), 'v': jax.random.normal(ks[2], (B, LKV, IMG_MODEL), jnp.float32), 'Wq': jax.random.normal(ks[3], (D_MODEL, D_MODEL), jnp.float32) * s_dm, 'bq': jnp.zeros((D_MODEL,), jnp.float32), 'Wk': jax.random.normal(ks[4], (IMG_MODEL, D_MODEL), jnp.float32) * s_im, 'bk': jnp.zeros((D_MODEL,), jnp.float32), 'Wv': jax.random.normal(ks[5], (IMG_MODEL, D_MODEL), jnp.float32) * s_im, 'bv': jnp.zeros((D_MODEL,), jnp.float32), 'Wo': jax.random.normal(ks[6], (D_MODEL, D_MODEL), jnp.float32) * s_dm, 'bo': jnp.zeros((D_MODEL,), jnp.float32)}
    _L1_xattn_all = _L1_xattn_setup()
    _L1_xattn_in = {k: v for k, v in _L1_xattn_all.items() if k in ('Wq', 'bq', 'Wk', 'bk', 'Wv', 'bv', 'Wo', 'bo')}
    del _L1_xattn_all

    def _L1_ffn_setup():
        import jax, jax.numpy as jnp
        import numpy as np
        import math
        B, T, D, H, E, TOPK, CAPF = (4, 256, 128, 16, 8, 2, 2.0)
        HD = D // H

        def layernorm(x, g, b, eps=1e-05):
            m = jnp.mean(x, -1, keepdims=True)
            v = jnp.mean(jnp.square(x - m), -1, keepdims=True)
            return (x - m) * jax.lax.rsqrt(v + eps) * g + b

        def block_forward(x, ln1_g, ln1_b, Wqkv, Wproj, ln2_g, ln2_b, Wgate, W1, b1, W2, b2):
            Bb, Tt, d = x.shape
            hd = HD
            half = hd // 2
            h = layernorm(x, ln1_g, ln1_b)
            qkv = (h @ Wqkv).reshape(Bb, Tt, H, 3 * hd)
            q, k, v = (qkv[..., :hd], qkv[..., hd:2 * hd], qkv[..., 2 * hd:])
            inv_freq = 1.0 / 10000.0 ** (jnp.arange(0, hd, 2, dtype=jnp.float32) / hd)
            ang = jnp.arange(Tt, dtype=jnp.float32)[:, None] * inv_freq
            sin = jnp.sin(ang)[None, :, None, :].astype(x.dtype)
            cos = jnp.cos(ang)[None, :, None, :].astype(x.dtype)

            def rope(t):
                t1, t2 = (t[..., :half], t[..., half:])
                return jnp.concatenate([t1 * cos - t2 * sin, t1 * sin + t2 * cos], -1)
            q, k = (rope(q), rope(k))
            scores = jnp.einsum('bqhd,bkhd->bhqk', q, k) / math.sqrt(hd)
            causal = jnp.tril(jnp.ones((Tt, Tt), dtype=bool))
            scores = jnp.where(causal, scores, jnp.asarray(-1000000000.0, scores.dtype))
            probs = jax.nn.softmax(scores, axis=-1)
            attn = jnp.einsum('bhqk,bkhd->bqhd', probs, v).reshape(Bb, Tt, d) @ Wproj
            x = x + attn
            h2 = layernorm(x, ln2_g, ln2_b)
            flat = h2.reshape(-1, d)
            N = flat.shape[0]
            capacity = int(math.ceil(CAPF * N / E))
            gates = jax.nn.softmax((flat @ Wgate).astype(jnp.float32), -1).astype(flat.dtype)
            _, top_inds = jax.lax.top_k(gates, TOPK)
            mask = jnp.zeros((N, E), dtype=bool).at[jnp.arange(N)[:, None], top_inds].set(True)
            pos = jnp.cumsum(mask.astype(jnp.int32), axis=0) * mask - 1
            keep = (pos < capacity) & mask
            t_flat = jnp.repeat(jnp.arange(N), TOPK)
            e_flat = top_inds.reshape(-1)
            p = pos[t_flat, e_flat]
            kp = keep[t_flat, e_flat]
            p_eff = jnp.where(kp, p, capacity)
            exp_in = jnp.zeros((E, capacity, d), flat.dtype).at[e_flat, p_eff].set(flat[t_flat], mode='drop')
            hmid = jax.nn.gelu(jnp.einsum('ecd,edf->ecf', exp_in, W1) + b1[:, None, :], approximate=False)
            exp_out = jnp.einsum('ecf,efd->ecd', hmid, W2) + b2[:, None, :]
            gate = gates[t_flat, e_flat] * kp.astype(flat.dtype)
            p_g = jnp.minimum(p_eff, capacity - 1)
            moe = jnp.zeros((N, d), flat.dtype).at[t_flat].add(exp_out[e_flat, p_g] * gate[:, None])
            return x + moe.reshape(Bb, Tt, d)
        key = jax.random.key(seed)
        ks = jax.random.split(key, 8)
        s = 0.02
        return {'x': jax.random.normal(ks[0], (B, T, D), jnp.float32), 'ln1_g': jnp.ones((D,), jnp.float32), 'ln1_b': jnp.zeros((D,), jnp.float32), 'Wqkv': jax.random.normal(ks[1], (D, 3 * D), jnp.float32) * s, 'Wproj': jax.random.normal(ks[2], (D, D), jnp.float32) * s, 'ln2_g': jnp.ones((D,), jnp.float32), 'ln2_b': jnp.zeros((D,), jnp.float32), 'Wgate': jax.random.normal(ks[3], (D, E), jnp.float32) * s, 'W1': jax.random.normal(ks[4], (E, D, 4 * D), jnp.float32) * s, 'b1': jnp.zeros((E, 4 * D), jnp.float32), 'W2': jax.random.normal(ks[5], (E, 4 * D, D), jnp.float32) * s, 'b2': jnp.zeros((E, D), jnp.float32)}
    _L1_ffn_all = _L1_ffn_setup()
    _L1_ffn_in = {k: v for k, v in _L1_ffn_all.items() if k in ('ln1_g', 'ln1_b', 'Wqkv', 'Wproj', 'ln2_g', 'ln2_b', 'Wgate', 'W1', 'b1', 'W2', 'b2')}
    del _L1_ffn_all
    return {'x': x, 'ctx_512': ctx_512, 'L0_xattn_Wk': _L0_xattn_in['Wk'], 'L0_xattn_bk': _L0_xattn_in['bk'], 'L0_xattn_Wq': _L0_xattn_in['Wq'], 'L0_xattn_bq': _L0_xattn_in['bq'], 'L0_xattn_Wv': _L0_xattn_in['Wv'], 'L0_xattn_bv': _L0_xattn_in['bv'], 'L0_xattn_Wck': _L0_xattn_in['Wck'], 'L0_xattn_bck': _L0_xattn_in['bck'], 'L0_xattn_Wcq': _L0_xattn_in['Wcq'], 'L0_xattn_bcq': _L0_xattn_in['bcq'], 'L0_xattn_Wcv': _L0_xattn_in['Wcv'], 'L0_xattn_bcv': _L0_xattn_in['bcv'], 'L0_xattn_Wp': _L0_xattn_in['Wp'], 'L0_xattn_bp': _L0_xattn_in['bp'], 'L0_ffn_router_w': _L0_ffn_in['router_w'], 'L0_ffn_w1_w': _L0_ffn_in['w1_w'], 'L0_ffn_w1_b': _L0_ffn_in['w1_b'], 'L0_ffn_w2_w': _L0_ffn_in['w2_w'], 'L0_ffn_w2_b': _L0_ffn_in['w2_b'], 'L0_ffn_wg_w': _L0_ffn_in['wg_w'], 'L0_ffn_wg_b': _L0_ffn_in['wg_b'], 'L1_xattn_Wq': _L1_xattn_in['Wq'], 'L1_xattn_bq': _L1_xattn_in['bq'], 'L1_xattn_Wk': _L1_xattn_in['Wk'], 'L1_xattn_bk': _L1_xattn_in['bk'], 'L1_xattn_Wv': _L1_xattn_in['Wv'], 'L1_xattn_bv': _L1_xattn_in['bv'], 'L1_xattn_Wo': _L1_xattn_in['Wo'], 'L1_xattn_bo': _L1_xattn_in['bo'], 'L1_ffn_ln1_g': _L1_ffn_in['ln1_g'], 'L1_ffn_ln1_b': _L1_ffn_in['ln1_b'], 'L1_ffn_Wqkv': _L1_ffn_in['Wqkv'], 'L1_ffn_Wproj': _L1_ffn_in['Wproj'], 'L1_ffn_ln2_g': _L1_ffn_in['ln2_g'], 'L1_ffn_ln2_b': _L1_ffn_in['ln2_b'], 'L1_ffn_Wgate': _L1_ffn_in['Wgate'], 'L1_ffn_W1': _L1_ffn_in['W1'], 'L1_ffn_b1': _L1_ffn_in['b1'], 'L1_ffn_W2': _L1_ffn_in['W2'], 'L1_ffn_b2': _L1_ffn_in['b2']}

def reference(x, ctx_512, L0_xattn_Wk, L0_xattn_bk, L0_xattn_Wq, L0_xattn_bq, L0_xattn_Wv, L0_xattn_bv, L0_xattn_Wck, L0_xattn_bck, L0_xattn_Wcq, L0_xattn_bcq, L0_xattn_Wcv, L0_xattn_bcv, L0_xattn_Wp, L0_xattn_bp, L0_ffn_router_w, L0_ffn_w1_w, L0_ffn_w1_b, L0_ffn_w2_w, L0_ffn_w2_b, L0_ffn_wg_w, L0_ffn_wg_b, L1_xattn_Wq, L1_xattn_bq, L1_xattn_Wk, L1_xattn_bk, L1_xattn_Wv, L1_xattn_bv, L1_xattn_Wo, L1_xattn_bo, L1_ffn_ln1_g, L1_ffn_ln1_b, L1_ffn_Wqkv, L1_ffn_Wproj, L1_ffn_ln2_g, L1_ffn_ln2_b, L1_ffn_Wgate, L1_ffn_W1, L1_ffn_b1, L1_ffn_W2, L1_ffn_b2):
    import jax
    import jax.numpy as jnp

    def _L0_xattn_ref(x, cross_input, Wk, bk, Wq, bq, Wv, bv, Wck, bck, Wcq, bcq, Wcv, bcv, Wp, bp):
        import jax, jax.numpy as jnp
        import numpy as np
        B, T, TC, C, CC, H = (2, 256, 64, 128, 64, 16)
        D = C // H

        def _heads(t):
            b, l, _ = t.shape
            return t.reshape(b, l, H, D).transpose(0, 2, 1, 3)
        scale = np.float32(1.0 / np.sqrt(D))
        q = _heads(x @ Wq + bq)
        k = _heads(x @ Wk + bk)
        v = _heads(x @ Wv + bv)
        att = jnp.einsum('bhqd,bhkd->bhqk', q, k) * scale
        causal = jnp.tril(jnp.ones((T, T), bool))
        att = jnp.where(causal[None, None], att, -jnp.inf)
        y = jnp.einsum('bhqk,bhkd->bhqd', jax.nn.softmax(att, axis=-1), v)
        qc = _heads(x @ Wcq + bcq)
        kc = _heads(cross_input @ Wck + bck)
        vc = _heads(cross_input @ Wcv + bcv)
        attc = jnp.einsum('bhqd,bhkd->bhqk', qc, kc) * scale
        y = y + jnp.einsum('bhqk,bhkd->bhqd', jax.nn.softmax(attc, axis=-1), vc)
        y = y.transpose(0, 2, 1, 3).reshape(x.shape[0], T, C)
        return y @ Wp + bp

    def _L0_ffn_ref(x, router_w, w1_w, w1_b, w2_w, w2_b, wg_w, wg_b):
        import jax, jax.numpy as jnp
        import numpy as np
        B, S, D, F, E, K = (4, 256, 128, 512, 8, 2)
        probs = jax.nn.softmax(jnp.einsum('bsd,ed->bse', x, router_w), axis=-1)
        token_probs, probs_idx = jax.lax.top_k(probs, K)
        gates = jnp.sum(token_probs[..., None] * jax.nn.one_hot(probs_idx, E, dtype=x.dtype), axis=-2)
        gates_e = jnp.moveaxis(gates, -1, 0)

        def body(acc, params):
            w1w, w1b, w2w, w2b, wgw, wgb, g = params
            y = jax.nn.gelu(jnp.einsum('bsd,fd->bsf', x, wgw) + wgb, approximate=False)
            h = y * (jnp.einsum('bsd,fd->bsf', x, w1w) + w1b)
            out = jnp.einsum('bsf,df->bsd', h, w2w) + w2b
            return (acc + out * g[..., None], None)
        acc0 = jnp.zeros_like(x)
        out, _ = jax.lax.scan(body, acc0, (w1_w, w1_b, w2_w, w2_b, wg_w, wg_b, gates_e))
        return out

    def _L1_xattn_ref(q, k, v, Wq, bq, Wk, bk, Wv, bv, Wo, bo):
        import jax, jax.numpy as jnp
        import numpy as np
        HEADS = 16
        D_MODEL = 128
        IMG_MODEL = 64
        D_K = D_MODEL // HEADS
        B, LQ, _ = q.shape
        LKV = k.shape[1]
        qh = (q @ Wq + bq).reshape(B, LQ, HEADS, D_K).transpose(0, 2, 1, 3)
        kh = (k @ Wk + bk).reshape(B, LKV, HEADS, D_K).transpose(0, 2, 1, 3)
        vh = (v @ Wv + bv).reshape(B, LKV, HEADS, D_K).transpose(0, 2, 1, 3)
        scale = 1.0 / np.sqrt(D_K)
        scores = jnp.einsum('bhqd,bhkd->bhqk', qh, kh) * scale
        attn = jax.nn.softmax(scores, axis=-1)
        out = jnp.einsum('bhqk,bhkd->bhqd', attn, vh)
        concat = out.transpose(0, 2, 1, 3).reshape(B, LQ, D_MODEL)
        return concat @ Wo + bo

    def _L1_ffn_ref(x, ln1_g, ln1_b, Wqkv, Wproj, ln2_g, ln2_b, Wgate, W1, b1, W2, b2):
        import jax, jax.numpy as jnp
        import numpy as np
        import math
        B, T, D, H, E, TOPK, CAPF = (4, 256, 128, 16, 8, 2, 2.0)
        HD = D // H

        def layernorm(x, g, b, eps=1e-05):
            m = jnp.mean(x, -1, keepdims=True)
            v = jnp.mean(jnp.square(x - m), -1, keepdims=True)
            return (x - m) * jax.lax.rsqrt(v + eps) * g + b

        def block_forward(x, ln1_g, ln1_b, Wqkv, Wproj, ln2_g, ln2_b, Wgate, W1, b1, W2, b2):
            Bb, Tt, d = x.shape
            hd = HD
            half = hd // 2
            h = layernorm(x, ln1_g, ln1_b)
            qkv = (h @ Wqkv).reshape(Bb, Tt, H, 3 * hd)
            q, k, v = (qkv[..., :hd], qkv[..., hd:2 * hd], qkv[..., 2 * hd:])
            inv_freq = 1.0 / 10000.0 ** (jnp.arange(0, hd, 2, dtype=jnp.float32) / hd)
            ang = jnp.arange(Tt, dtype=jnp.float32)[:, None] * inv_freq
            sin = jnp.sin(ang)[None, :, None, :].astype(x.dtype)
            cos = jnp.cos(ang)[None, :, None, :].astype(x.dtype)

            def rope(t):
                t1, t2 = (t[..., :half], t[..., half:])
                return jnp.concatenate([t1 * cos - t2 * sin, t1 * sin + t2 * cos], -1)
            q, k = (rope(q), rope(k))
            scores = jnp.einsum('bqhd,bkhd->bhqk', q, k) / math.sqrt(hd)
            causal = jnp.tril(jnp.ones((Tt, Tt), dtype=bool))
            scores = jnp.where(causal, scores, jnp.asarray(-1000000000.0, scores.dtype))
            probs = jax.nn.softmax(scores, axis=-1)
            attn = jnp.einsum('bhqk,bkhd->bqhd', probs, v).reshape(Bb, Tt, d) @ Wproj
            x = x + attn
            h2 = layernorm(x, ln2_g, ln2_b)
            flat = h2.reshape(-1, d)
            N = flat.shape[0]
            capacity = int(math.ceil(CAPF * N / E))
            gates = jax.nn.softmax((flat @ Wgate).astype(jnp.float32), -1).astype(flat.dtype)
            _, top_inds = jax.lax.top_k(gates, TOPK)
            mask = jnp.zeros((N, E), dtype=bool).at[jnp.arange(N)[:, None], top_inds].set(True)
            pos = jnp.cumsum(mask.astype(jnp.int32), axis=0) * mask - 1
            keep = (pos < capacity) & mask
            t_flat = jnp.repeat(jnp.arange(N), TOPK)
            e_flat = top_inds.reshape(-1)
            p = pos[t_flat, e_flat]
            kp = keep[t_flat, e_flat]
            p_eff = jnp.where(kp, p, capacity)
            exp_in = jnp.zeros((E, capacity, d), flat.dtype).at[e_flat, p_eff].set(flat[t_flat], mode='drop')
            hmid = jax.nn.gelu(jnp.einsum('ecd,edf->ecf', exp_in, W1) + b1[:, None, :], approximate=False)
            exp_out = jnp.einsum('ecf,efd->ecd', hmid, W2) + b2[:, None, :]
            gate = gates[t_flat, e_flat] * kp.astype(flat.dtype)
            p_g = jnp.minimum(p_eff, capacity - 1)
            moe = jnp.zeros((N, d), flat.dtype).at[t_flat].add(exp_out[e_flat, p_g] * gate[:, None])
            return x + moe.reshape(Bb, Tt, d)
        return block_forward(x, ln1_g, ln1_b, Wqkv, Wproj, ln2_g, ln2_b, Wgate, W1, b1, W2, b2)
    x = x + _L0_xattn_ref(_layernorm(x, axis=-1), ctx_512, L0_xattn_Wk, L0_xattn_bk, L0_xattn_Wq, L0_xattn_bq, L0_xattn_Wv, L0_xattn_bv, L0_xattn_Wck, L0_xattn_bck, L0_xattn_Wcq, L0_xattn_bcq, L0_xattn_Wcv, L0_xattn_bcv, L0_xattn_Wp, L0_xattn_bp)
    x = x + _L0_ffn_ref(_layernorm(x, axis=-1), L0_ffn_router_w, L0_ffn_w1_w, L0_ffn_w1_b, L0_ffn_w2_w, L0_ffn_w2_b, L0_ffn_wg_w, L0_ffn_wg_b)
    x = x + _L1_xattn_ref(_layernorm(x, axis=-1), ctx_512, ctx_512, L1_xattn_Wq, L1_xattn_bq, L1_xattn_Wk, L1_xattn_bk, L1_xattn_Wv, L1_xattn_bv, L1_xattn_Wo, L1_xattn_bo)
    x = x + _L1_ffn_ref(_layernorm(x, axis=-1), L1_ffn_ln1_g, L1_ffn_ln1_b, L1_ffn_Wqkv, L1_ffn_Wproj, L1_ffn_ln2_g, L1_ffn_ln2_b, L1_ffn_Wgate, L1_ffn_W1, L1_ffn_b1, L1_ffn_W2, L1_ffn_b2)
    return x

_drawn_inputs = setup_inputs


def setup_inputs(seed=0):
    import zlib

    import numpy as np

    out = dict(_drawn_inputs(seed))
    spreads = {'L0_xattn_bk': (0.0, 0.8),
     'L0_xattn_bq': (0.0, 0.499),
     'L0_xattn_bv': (0.0, 0.1),
     'L0_xattn_bck': (0.0, 0.8),
     'L0_xattn_bcq': (0.0, 0.422),
     'L0_xattn_bcv': (0.0, 0.1),
     'L0_xattn_bp': (0.0, 0.1),
     'L1_xattn_bq': (0.0, 0.441),
     'L1_xattn_bk': (0.0, 0.8),
     'L1_xattn_bv': (0.0, 0.1),
     'L1_xattn_bo': (0.0, 0.1),
     'L1_ffn_ln1_g': (1.0, 0.6),
     'L1_ffn_ln1_b': (0.0, 0.8),
     'L1_ffn_ln2_g': (1.0, 0.6),
     'L1_ffn_ln2_b': (0.0, 0.8),
     'L1_ffn_b1': (0.0, 0.8),
     'L1_ffn_b2': (0.0, 0.8)}
    factors = {'L0_ffn_router_w': 8.0,
     'L0_ffn_w1_w': 8.0,
     'L0_ffn_w1_b': 8.0,
     'L0_ffn_w2_w': 8.0,
     'L0_ffn_w2_b': 8.0,
     'L0_ffn_wg_w': 8.0,
     'L0_ffn_wg_b': 8.0,
     'L1_ffn_Wqkv': 4.224,
     'L1_ffn_Wproj': 4.224,
     'L1_ffn_Wgate': 5.798,
     'L1_ffn_W1': 8.0,
     'L1_ffn_W2': 8.0}
    for name, (base, spread) in spreads.items():
        noise = np.random.default_rng([zlib.crc32(name.encode()), seed]).standard_normal(out[name].shape)
        drawn = base * np.exp(spread * noise) if base else spread * noise
        out[name] = jnp.asarray(drawn.astype(out[name].dtype))
    for name, factor in factors.items():
        out[name] = (out[name] * factor).astype(out[name].dtype)
    return out
```

```python
from contextlib import ExitStack

import concourse.bass as bass
from concourse import mybir

F32 = mybir.dt.float32
BF16 = mybir.dt.bfloat16
ALU = mybir.AluOpType
ACT = mybir.ActivationFunctionType
AX = mybir.AxisListType


class Item:

    def __init__(self, kind, ch, p, banks, frees):
        self.kind, self.ch, self.p, self.banks, self.frees = kind, ch, p, banks, frees


class Part:

    def __init__(self, cross=0, self_=0, affine=False, vbias=False, projs="", weights=(), stores=(), wo=None,
                 resid_bias=False, gated=False, capacity=False):
        self.cross, self.self_, self.affine, self.vbias = cross, self_, affine, vbias
        self.projs, self.weights, self.stores, self.wo = projs, weights, stores, wo
        self.resid_bias, self.gated, self.capacity = resid_bias, gated, capacity


P = 128
B = 16
T = 256
C = 128
TILES = B * T // P
TOK = B * T
H = 16
D = C // H
TC = 1601
CC = 64
SCALE = float(D) ** -0.5
KT = (TC + P - 1) // P
KLAST = TC - (KT - 1) * P
QUADS = H // 4
TERMS_Q = (0, 0, 0, 1, 1, 2)
TERMS_K = (0, 1, 2, 0, 1, 0)
ROWS = 6 * D
ROWSM = ROWS + 3
SC = 401
SSTART = (0, SC, 2 * SC, TC - SC)
VC = 32
E = 8
F = 512
FC = F // P
CAP = 1024
EPS = 1e-5
MASKED = -1.0e30
CHUNKS = TOK // 512
KCH = ((0, 401), (401, 401), (802, 401), (1203, 398))


def lin(b, per, c):
    return b * per + c


def build(nc, A, out):
    ctx = ExitStack()
    with ctx:
        def sb(name, shape, dt=F32):
            return ctx.enter_context(nc.sbuf_tensor(name, shape, dt))

        def sem(name):
            if name not in sems:
                sems[name] = ctx.enter_context(nc.semaphore(name))
            return sems[name]

        sems = {}

        def scratch(name, shape, dt):
            return nc.dram_tensor(name, shape, dt).ap()

        x = sb("x", [P, TOK])
        xnT = sb("xnT", [P, TOK])
        arenaA = sb("arenaA", [P, 12288])
        arenaB = sb("arenaB", [P, 12992])
        ident = sb("ident", [P, P])
        ident16 = sb("ident16", [P, P], BF16)
        mask_qk = sb("mask_qk", [P, P], BF16)
        mask_kq = sb("mask_kq", [P, P], BF16)
        upper = sb("upper", [P, P])
        ones = sb("ones", [P, P])
        rank = sb("rank", [P, TILES, E])
        stat = sb("stat", [P, 4, TILES])
        kst = sb("kst", [P, QUADS, 2, TC], BF16)
        kss = sb("kss", [P, QUADS, 2, T], BF16)
        vq = sb("vq", [P, 2, KT, 4, VC])
        vs = sb("vs", [P, 2, 2, 4, VC])
        vb = sb("vb", [P, KT, C])
        osb = sb("osb", [P, 2 * T])
        yb = sb("yb", [P, 2, C])
        yb2 = sb("yb2", [P, 2, C])
        yT = sb("yT", [P, T])
        rec = sb("rec", [P, 16])
        mp = sb("mp", [P, 2, 2, 2, 4])
        mps = sb("mps", [P, 2, 3, 4])
        mx = sb("mx", [P, 2, 2, 4])
        mr = sb("mr", [P, 2, 2, 4])
        mpt = sb("mpt", [P, 48], BF16)
        mrow = sb("mrow", [P, 2, T], BF16)
        pick = sb("pick", [P, 2, 2, P], BF16)
        wbig = sb("wbig", [P, 6, C])
        wkv = sb("wkv", [P, 2, C])
        colv = sb("colv", [P, 4])
        rowv = sb("rowv", [P, 2, C])
        rope = sb("rope", [P, 2, T])
        b1s = sb("b1s", [P, 2, E, FC])
        b2s = sb("b2s", [E, C])
        rw = sb("rw", [P, E])
        gate = osb[:, 0:TILES * E].rearrange("p (t e) -> p t e", e=E)
        gch = osb[:, TILES * E:TILES * E + 4 * E].rearrange("p (t e) -> p t e", e=E)

        psum = ctx.enter_context(nc.psum_tensor("psum", [P, 8, 512], F32))

        p_ring = arenaA[:, 0:4096].rearrange("p (s j n) -> p s j n", s=4, j=4)
        v_self = arenaA[:, 8192:12288]
        qst, qss = (arenaA[:, lo:lo + 2048].bitcast(BF16).rearrange("p (g j e n) -> p g j e n", g=QUADS, j=2, e=2)
                    for lo in (4096, 6144))
        xn = arenaB[:, 0:4096]
        sq = arenaB[:, 4096:8192]
        q_parts = [arenaB[:, 4096 + 768 * i:4096 + 768 * (i + 1)].bitcast(BF16).rearrange("p (a n) -> p a n", a=3)
                   for i in range(4)]
        q_res = [arenaB[:, 7168 + 512 * i:7168 + 512 * (i + 1)] for i in range(4)]
        q_x32 = [arenaB[:, 9216 + 512 * i:9216 + 512 * (i + 1)] for i in range(4)]
        q_t1 = arenaB[:, 11264:11776]
        q_t2 = arenaB[:, 11776:12288]
        cx = [arenaB[:, TC * i:TC * (i + 1)] for i in range(2)]
        at = 2 * TC
        k_res = [arenaB[:, at + SC * i:at + SC * (i + 1)] for i in range(4)]
        at += 4 * SC
        k_parts = [arenaB[:, at + 2402 * i:at + 2402 * (i + 1)].bitcast(BF16)[:, 0:3 * TC].rearrange(
            "p (a n) -> p a n", a=3) for i in range(2)]
        at += 2 * 2402
        v_st = [arenaB[:, at + KT * C * i:at + KT * C * (i + 1)].rearrange("p (t c) -> p t c", t=KT) for i in range(2)]
        at += 2 * KT * C
        assert at <= 12992

        kx_d = scratch("kx_d", [B, H, 3, D, TC], BF16)
        vx_d = scratch("vx_d", [B, TC, C], F32)
        qx_d = scratch("qx_d", [H, ROWSM, TOK], BF16)
        qs_d = scratch("qs_d", [H, ROWSM, TOK], BF16)
        ks_d = scratch("ks_d", [H, ROWS, TOK], BF16)
        res_d = scratch("res_d", [P, TILES, C], F32)
        res = arenaB[:, 8192:12288]

        phase_done = sem("phase_done")
        loaded = sem("loaded")
        made = sem("made")

        count = {}

        waited = sem("waited")

        def pool_wait(pool, sm, value):
            pool.wait_ge(sm, value)
            if not isinstance(value, int):
                pool.sem_inc(waited, 1)

        def phase_end(eng, name):
            count[name] = count.get(name, 0) + 1
            eng.drain().then_inc(phase_done, 1)
            eng.wait_ge(phase_done, 5 * count[name])

        class ln_s:
            dve, act = sem("ln_dve"), sem("ln_act")


        x3 = x[:, :].rearrange("p (t c) -> p t c", c=C)
        xn3 = xn.rearrange("p (t c) -> p t c", c=C)
        sq3 = sq.rearrange("p (t c) -> p t c", c=C)

        def ln_dve(dve, k):
            s = ln_s
            dve.tensor_reduce(stat[:, 0, :], x3, AX.X, ALU.add).then_inc(s.dve, 1)
            dve.wait_ge(s.dve, 6 * k + 1)
            dve.tensor_scalar(stat[:, 1, :], stat[:, 0, :], 1.0 / C, None, ALU.mult).then_inc(s.dve, 1)
            dve.wait_ge(s.dve, 6 * k + 2)
            dve.tensor_tensor(xn3, x3, stat[:, 1, :].unsqueeze(2).to_broadcast([P, TILES, C]),
                              ALU.subtract).then_inc(s.dve, 1)
            dve.wait_ge(s.act, 2 * k + 1)
            dve.tensor_reduce(stat[:, 2, :], sq3, AX.X, ALU.add).then_inc(s.dve, 1)
            dve.wait_ge(s.act, 2 * k + 2)
            dve.reciprocal(stat[:, 1, :], stat[:, 3, :]).then_inc(s.dve, 1)
            dve.wait_ge(s.dve, 6 * k + 5)
            dve.tensor_tensor(xn3, xn3, stat[:, 1, :].unsqueeze(2).to_broadcast([P, TILES, C]),
                              ALU.mult).then_inc(s.dve, 1)

        def ln_act(act, k):
            s = ln_s
            act.wait_ge(s.dve, 6 * k + 3)
            act.activation(sq, xn, ACT.Square).then_inc(s.act, 1)
            act.wait_ge(s.dve, 6 * k + 4)
            act.activation(stat[:, 3, :], stat[:, 2, :], ACT.Sqrt, bias=eps_col[:, 0:1], scale=1.0 / C).then_inc(s.act, 1)

        eps_col = sb("eps_col", [P, 1])

        def proj_plan(c):
            order = [("T", 0)]
            for ch in range(CHUNKS):
                if ch + 1 < CHUNKS:
                    order.append(("T", ch + 1))
                order += [(kind, ch, p) for p, kind in enumerate(c.projs)]
            items, bank, owner = [], 0, [None] * 8
            nact = ndve = nq = 0
            for it in order:
                kind = it[0]
                n = 2 if kind == "R" else 1
                if n == 2 and bank % 2:
                    bank += 1
                banks = [(bank + k) % 8 for k in range(n)]
                bank += n
                o = Item(kind=kind, ch=it[1], p=it[2] if len(it) > 2 else None, banks=banks,
                                    frees=[owner[k] for k in banks if owner[k]])
                if kind == "T":
                    nact += 1
                    o.t = nact
                    mine = ("act", nact)
                else:
                    ndve += 1
                    mine = ("dve", ndve)
                    if kind in "QR":
                        o.q = nq
                        nq += 1
                for k in banks:
                    owner[k] = mine
                o.freed = mine[1]
                items.append(o)
            return items

        def proj_sems(n, c):
            class r:
                filled, act, dve = sem(n + "_pj_filled"), sem(n + "_pj_act"), sem(n + "_pj_dve")

            if c.stores:
                r.mid, r.low = sem(n + "_pj_mid"), sem(n + "_pj_low")
                r.stored = [sem(f"{n}_pj_stored{i}") for i in range(4)]
                if "R" in c.projs:
                    r.rp = sem(n + "_pj_rope")
                else:
                    r.high = sem(n + "_pj_high")
            return r

        def proj_pe(pe, c):
            for i, o in enumerate(c.items):
                for who, v in o.frees:
                    pe.wait_ge(c.pj.act if who == "act" else c.pj.dve, v)
                bk = psum[:, o.banks[0], :]
                if o.kind == "T":
                    for t in range(4):
                        k = 4 * o.ch + t
                        last = pe.transpose(bk[:, t * P:(t + 1) * P], xn[:, k * P:(k + 1) * P], ident[:, :])
                else:
                    pe.wait_ge(c.pj.act, o.ch + 1)
                    src = xnT[:, o.ch * 512:(o.ch + 1) * 512]
                    w = c.weights[o.p]
                    if o.kind == "Q":
                        last = pe.matmul(bk, w[0], src, start=True, stop=True)
                    elif o.kind == "R":
                        pe.matmul(bk, w[0], src, start=True, stop=True)
                        last = pe.matmul(psum[:, o.banks[1], :], w[1], src, start=True, stop=True)
                    else:
                        n = C if o.kind == "V" else E
                        for t in range(4):
                            last = pe.matmul(bk[:, t * n:(t + 1) * n], src[:, t * P:(t + 1) * P], w[0],
                                             start=True, stop=True)
                last.then_inc(c.pj.filled, 1)

        def proj_act(act, c):
            for i, o in enumerate(c.items):
                bk = psum[:, o.banks[0], :]
                if o.kind == "T":
                    act.wait_ge(c.pj.filled, i + 1)
                    dst = xnT[:, o.ch * 512:(o.ch + 1) * 512]
                    if c.affine:
                        act.activation(dst, bk, ACT.Identity, bias=colv[:, 3:4], scale=colv[:, 2:3]).then_inc(c.pj.act, 1)
                    else:
                        act.activation(dst, bk, ACT.Copy).then_inc(c.pj.act, 1)
                elif o.kind == "Q":
                    act.wait_ge(c.pj.filled, i + 1)
                    if o.q >= 4:
                        act.wait_ge(c.pj.stored[o.q % 4], 96 * (o.q // 4))
                    act.activation(q_parts[o.q % 4][:, 0, :], bk, ACT.Identity,
                                   bias=colv[:, o.p:o.p + 1]).then_inc(c.pj.high, 1)

        def proj_dve(dve, c):
            rp = 0
            pending = []

            def low(o):
                dve.wait_ge(c.pj.mid, o.q + 1)
                dve.tensor_tensor(q_parts[o.q % 4][:, 2, :], q_res[o.q % 4], q_parts[o.q % 4][:, 1, :],
                                  ALU.subtract).then_inc(c.pj.low, 1)

            for i, o in enumerate(c.items):
                if o.kind == "T":
                    continue
                bk = psum[:, o.banks[0], :]
                dve.wait_ge(c.pj.filled, i + 1)
                if o.kind == "Q":
                    dve.wait_ge(c.pj.high, o.q + 1)
                    if o.q >= 4:
                        dve.wait_ge(c.pj.low, o.q - 3)
                    dve.scalar_tensor_tensor(q_res[o.q % 4], bk, colv[:, o.p:o.p + 1], q_parts[o.q % 4][:, 0, :],
                                             ALU.add, ALU.subtract).then_inc(c.pj.dve, 1)
                    pending.append(o)
                elif o.kind == "R":
                    view = lambda a: a.rearrange("p (b t) -> p b t", b=2)
                    tab = lambda k: rope[:, k, :].unsqueeze(1).to_broadcast([P, 2, T])
                    x32 = q_x32[o.q % 4]
                    dve.wait_ge(c.pj.rp, rp)
                    dve.tensor_tensor(view(q_t1), view(bk), tab(0), ALU.mult).then_inc(c.pj.rp, 1)
                    dve.tensor_tensor(view(q_t2), view(psum[:, o.banks[1], :]), tab(1), ALU.mult).then_inc(c.pj.rp, 1)
                    dve.wait_ge(c.pj.rp, rp + 2)
                    dve.tensor_tensor(x32, q_t1, q_t2, ALU.add).then_inc(c.pj.rp, 1)
                    dve.wait_ge(c.pj.rp, rp + 3)
                    if o.q >= 4:
                        dve.wait_ge(c.pj.stored[o.q % 4], 96 * (o.q // 4))
                    dve.tensor_copy(q_parts[o.q % 4][:, 0, :], x32).then_inc(c.pj.rp, 1)
                    rp += 4
                    dve.wait_ge(c.pj.rp, rp)
                    if o.q >= 4:
                        dve.wait_ge(c.pj.low, o.q - 3)
                    dve.tensor_tensor(q_res[o.q % 4], x32, q_parts[o.q % 4][:, 0, :], ALU.subtract).then_inc(c.pj.dve, 1)
                    pending.append(o)
                elif o.kind == "V":
                    dst = v_self[:, o.ch * 512:(o.ch + 1) * 512]
                    if c.vbias:
                        dve.tensor_tensor(dst.rearrange("p (t c) -> p t c", t=4), bk.rearrange("p (t c) -> p t c", t=4),
                                          rowv[:, 1, :].unsqueeze(1).to_broadcast([P, 4, C]), ALU.add).then_inc(c.pj.dve, 1)
                    else:
                        dve.tensor_copy(dst, bk).then_inc(c.pj.dve, 1)
                else:
                    dve.tensor_copy(gate[:, 4 * o.ch:4 * o.ch + 4, :],
                                    bk[:, 0:4 * E].rearrange("p (t e) -> p t e", e=E)).then_inc(c.pj.dve, 1)
                if len(pending) > 1:
                    low(pending.pop(0))
            for o in pending:
                low(o)

        def proj_pool(pool, c):
            for o in c.items:
                if o.kind in "QR":
                    pool.wait_ge(c.pj.dve, o.freed)
                    pool.tensor_copy(q_parts[o.q % 4][:, 1, :], q_res[o.q % 4]).then_inc(c.pj.mid, 1)

        def proj_sp(sp, c):
            n = 0
            for o in c.items:
                if o.kind in "QR":
                    sp.wait_ge(c.pj.low, o.q + 1)
                    dst, terms = c.stores[o.p]
                    for t in range(6):
                        sp.dma_start(dst[:, D * t:D * (t + 1), o.ch * 512:(o.ch + 1) * 512],
                                     q_parts[o.q % 4][:, terms[t], :]).then_inc(c.pj.stored[o.q % 4], 16)
                    n = o.q + 1
            for i in range(4):
                if n > i:
                    sp.wait_ge(c.pj.stored[i], 96 * ((n - i + 3) // 4))

        def ctx_sems(n):
            class r:
                filled, high, vout = sem(n + "_filled"), sem(n + "_high"), sem(n + "_v")
                res, mid, low, one = sem(n + "_res"), sem(n + "_mid"), sem(n + "_low"), sem(n + "_one")
                loaded = sem(n + "_loaded0"), sem(n + "_loaded1")
                stored = sem(n + "_stored0"), sem(n + "_stored1")

            return r

        def pairs(eng, body):
            for r in range(2):
                body(0, r, True)
            with eng.Fori(1, B // 2) as i:
                for r in range(2):
                    body(i, r, False)

        def nth(c, i, per, k):
            return lin(i + 8 * c.turn, per, k) if c.turn else lin(i, per, k)

        def ctx_pe(pe, c):
            s = c.cx
            pe.wait_ge(s.one, 1 + c.turn)

            def body(i, r, first):
                pe.wait_ge(s.loaded[r], nth(c, i, 16, 16))
                for k, (k0, n) in enumerate(KCH):
                    if not (first and r == 0):
                        pe.wait_ge(s.res, nth(c, i, 8, 4 * r + k - 3))
                    pe.matmul(psum[:, k, 0:n], wkv[:, 0, :], cx[r][:, k0:k0 + n], start=True, stop=True).then_inc(s.filled, 1)
                for g in range(4):
                    if not (first and r == 0):
                        pe.wait_ge(s.vout, nth(c, i, 8, 4 * r + g - 3))
                    for t in range(4 * g, min(4 * g + 4, KT)):
                        m = P if t < KT - 1 else KLAST
                        last = pe.matmul(psum[0:m, 4 + g, (t % 4) * C:(t % 4 + 1) * C], cx[r][:, t * P:t * P + m],
                                         wkv[:, 1, :], start=True, stop=True)
                    last.then_inc(s.filled, 1)

            pairs(pe, body)

        def ctx_act(act, c):
            s = c.cx

            def body(i, r, first):
                if not first:
                    act.wait_ge(s.stored[r], nth(c, i, 80, 0))
                for k, (k0, n) in enumerate(KCH):
                    act.wait_ge(s.filled, nth(c, i, 16, 8 * r + k + 1))
                    act.activation(k_parts[r][:, 0, k0:k0 + n], psum[:, k, 0:n], ACT.Copy).then_inc(s.high, 1)
                for g in range(4):
                    act.wait_ge(s.filled, nth(c, i, 16, 8 * r + 4 + g + 1))
                    m, n = (P, 4) if g < 3 else (KLAST, 1)
                    act.activation(v_st[r][0:m, 4 * g:4 * g + n, :],
                                   psum[0:m, 4 + g, 0:n * C].rearrange("p (t c) -> p t c", c=C), ACT.Copy).then_inc(s.vout, 1)

            pairs(act, body)

        def ctx_dve(dve, c):
            s = c.cx

            def low(i, r, k):
                k0, n = KCH[k]
                dve.wait_ge(s.mid, nth(c, i, 8, 4 * r + k + 1))
                dve.tensor_tensor(k_parts[r][:, 2, k0:k0 + n], k_res[k][:, 0:n], k_parts[r][:, 1, k0:k0 + n],
                                  ALU.subtract).then_inc(s.low, 1)

            def body(i, r, first):
                for k, (k0, n) in enumerate(KCH):
                    dve.wait_ge(s.high, nth(c, i, 8, 4 * r + k + 1))
                    if not (first and r == 0):
                        dve.wait_ge(s.low, nth(c, i, 8, 4 * r + k - 3))
                    dve.tensor_tensor(k_res[k][:, 0:n], psum[:, k, 0:n], k_parts[r][:, 0, k0:k0 + n],
                                      ALU.subtract).then_inc(s.res, 1)
                    if k:
                        low(i, r, k - 1)
                low(i, r, 3)

            pairs(dve, body)

        def ctx_pool(pool, c):
            s = c.cx
            for rows, value in ((slice(CC, P), 0.0), (slice(CC, CC + 1), 1.0)):
                for r in range(2):
                    pool.memset(cx[r][rows, :], value).then_inc(made, 1)
                count["made"] += 2
                pool.wait_ge(made, count["made"])
            pool.sem_inc(s.one, 1)

            def body(i, r, first):
                for k, (k0, n) in enumerate(KCH):
                    pool_wait(pool, s.res, nth(c, i, 8, 4 * r + k + 1))
                    pool.tensor_copy(k_parts[r][:, 1, k0:k0 + n], k_res[k][:, 0:n]).then_inc(s.mid, 1)

            pairs(pool, body)

        def ctx_sp(sp, c):
            s = c.cx

            def load(i, r):
                if isinstance(i, int):
                    src = A["ctxT"][2 * i + r]
                else:
                    src = A["ctxT"][i * 2 + r]
                sp.dma_start(cx[r][0:CC, :], src).then_inc(s.loaded[r], 16)

            def store(i, r):
                b = i * 2 + r
                sp.wait_ge(s.low, nth(c, i, 8, 4 * r + 4))
                for p in range(3):
                    sp.dma_start(kx_d[b, :, p], k_parts[r][:, p, :]).then_inc(s.stored[r], 16)
                sp.wait_ge(s.vout, nth(c, i, 8, 4 * r + 4))
                full = (KT - 1) * P
                sp.dma_start(vx_d[b, 0:full].rearrange("(t p) c -> p t c", p=P), v_st[r][:, 0:KT - 1, :]).then_inc(s.stored[r], 16)
                sp.dma_start(vx_d[b, full:TC], v_st[r][0:KLAST, KT - 1, :]).then_inc(s.stored[r], 16)

            load(0, 0)
            load(0, 1)

            def body(i, last):
                for r in range(2):
                    if not last:
                        sp.wait_ge(s.filled, nth(c, i, 16, 8 * r + 8))
                        load(i + 1, r)
                    store(i, r)

            with sp.Fori(0, B // 2 - 1) as i:
                body(i, False)
            body(B // 2 - 1, True)
            for r in range(2):
                sp.wait_ge(s.stored[r], 80 * (B // 2) * (1 + c.turn))

        def attn_cfg(c, n):
            c.ns = c.cross + c.self_
            c.NG = KT * c.cross + 2 * c.self_
            c.NT = 2 * c.NG
            c.NS = 16 * c.cross + 4 * c.self_
            c.nm = 2 * c.ns
            c.nv = 2 * c.cross + c.self_

            class s:
                t_filled, p_ready, pv_done = sem(n + "_t_filled"), sem(n + "_p_ready"), sem(n + "_pv_done")
                s_filled, s_free, m_chain = sem(n + "_s_filled"), sem(n + "_s_free"), sem(n + "_m_chain")
                misc_filled, misc_done = sem(n + "_misc_filled"), sem(n + "_misc_done")
                o_evac, o_chain = sem(n + "_o_evac"), sem(n + "_o_chain")
                v_copied, v_loaded = sem(n + "_v_copied"), sem(n + "_v_loaded")

            s.kq_loaded = [sem(f"{n}_kq{g}") for g in range(QUADS)]
            s.m_loaded = [sem(f"{n}_ml{g}") for g in range(QUADS)] if c.cross else []
            c.at = s
            c.nkq = (6 + 2) * c.cross + 4 * c.self_
            c.M_OPS = c.cross + 2 * c.self_ + 4
            c.O_OPS = 2 if c.ns == 1 else 4

        def timeline(c, b, g):
            first, last = (isinstance(b, int) and b == 0), (isinstance(b, int) and b == B - 1)
            NT, NS = c.NT, c.NS
            when = [[] for _ in range(NT)]
            if c.cross:
                for k in range(c.M_OPS):
                    when[1 + k].append(("Ma", k))
                o_at = c.M_OPS + 6
                when[c.M_OPS + 3].append(("Mb",))
                when[o_at].append(("O",))
                for k in range(c.O_OPS + 1):
                    when[o_at + 2 + k].append(("N", k))
                when[o_at + c.O_OPS + 4].append(("Y",))
                when[o_at + c.O_OPS + 7].append(("PR",))
            else:
                when[0] += [("Ma", k) for k in range(c.M_OPS)]
                when[1].append(("Mb",))
                when[2] += [("O",)] + [("N", k) for k in range(c.O_OPS + 1)]
                when[3] += [("Y",), ("PR",)]
            ev, k = [], 0
            for i in range(NT):
                ev.append(("T", i // 2, i % 2))
                while k < (i + 1) * NS // NT:
                    if not (last and g >= 2):
                        ev.append(("S", k))
                    k += 1
                if i == 1 and not (first and g == 0):
                    ev += [("PVL",), ("OE",)]
                if i % 2 == 1 and i > 2:
                    ev.append(("PV", i // 2 - 1))
                for name in when[i]:
                    if name[0] in ("Ma", "Mb") and last and g == 3:
                        continue
                    if name[0] in "ON" and first and g == 0:
                        continue
                    if name[0] in ("Y", "PR") and (g != 0 or first):
                        continue
                    ev.append(name)
            return ev

        TAIL = [("PVL",), ("OE",), ("O",), ("Y",), ("PR",)]

        def misc_index(b, g, kind):
            if isinstance(b, int) and b == 0:
                return {"Mb": [1, 2, 4, 6][g], "O": [None, 3, 5, 7][g]}[kind]
            if g == 4:
                return lin(b, 10, -2 + 9 + ["O", "Y", "PR"].index(kind))
            if g == 0:
                return lin(b, 10, -2 + ["Mb", "O", "Y", "PR"].index(kind))
            off = 4 + 2 * (g - 1)
            if isinstance(b, int) and b == B - 1 and g == 3:
                return lin(b, 10, -2 + off)
            return lin(b, 10, -2 + off + (kind == "O"))

        def ahead(b, g, k):
            g2 = g + k
            return (b + g2 // 4 if g2 // 4 else b), g2 % 4

        def steps(eng, emit):
            for g in range(QUADS):
                emit(0, g)
            with eng.Fori(1, B - 1) as b:
                for g in range(QUADS):
                    emit(b, g)
            for g in range(QUADS):
                emit(B - 1, g)

        def misc_bank():
            return psum[:, 7, :]

        def seg(c, u):
            if u >= KT * c.cross:
                own = u - KT * c.cross
                return own, None, P, T - P * own
            return None, u, (P if u < KT - 1 else KLAST), T

        def attn_pe(pe, c):
            s = c.at

            def s_unit(b, g, k, n_is_zero_idx):
                idx_c = g * c.NS + k
                if k == 0:
                    pe.wait_ge(s.kq_loaded[g], lin(b, 16 * c.nkq, 16 * c.nkq))
                if not (isinstance(b, int) and b == 0 and idx_c < 2):
                    pe.wait_ge(s.s_free, lin(b, QUADS * c.NS, idx_c - 1))
                bk = 2 * (idx_c % 2)
                if c.cross and k < 16:
                    j, qt, half = k // 4, k // 2 % 2, k % 2
                    e, hp = j % 2, j // 2
                    for m in range(2):
                        k0 = SSTART[2 * half + m]
                        last = pe.matmul(psum[:, bk + m, 0:SC], qst[:, g, hp, e, qt * P:(qt + 1) * P],
                                         kst[:, g, hp, k0:k0 + SC], start=True, stop=True)
                else:
                    j = k - 16 * c.cross
                    e, hp = j % 2, j // 2
                    ps = psum[:, bk, :]
                    pe.matmul(ps[:, 0:P], qss[:, g, hp, e, 0:P], kss[:, g, hp, 0:P], start=True, stop=False,
                              skip_group_check=True)
                    pe.matmul(ps[:, 0:P], ident16[:, :], mask_qk[:, :], start=False, stop=True, skip_group_check=True)
                    pe.matmul(ps[:, P:3 * P], qss[:, g, hp, e, P:T], kss[:, g, hp, :], start=True, stop=False,
                              skip_group_check=True)
                    last = pe.matmul(ps[:, 2 * P:3 * P], ident16[:, :], mask_qk[:, :], start=False, stop=True,
                                     skip_group_check=True)
                last.then_inc(s.s_filled, 1)

            def t_unit(b, g, u, hp):
                idx_c = g * c.NT + 2 * u + hp
                if u == 0 and hp == 0:
                    if c.cross:
                        pe.wait_ge(s.m_loaded[g], lin(b, 16 * c.nm, 16 * c.nm))
                    elif isinstance(b, int) and b == 0 and g == 0:
                        pe.wait_ge(s.misc_done, 1)
                    else:
                        pe.wait_ge(s.misc_done, misc_index(*((b, g - 1) if g else (b - 1, 3)), "Mb") + 1)
                if not (isinstance(b, int) and b == 0 and idx_c < 2):
                    pe.wait_ge(s.p_ready, lin(b, QUADS * c.NT, idx_c - 1))
                own, t, m, n = seg(c, u)
                ps = psum[0:m, 4 + idx_c % 2, 0:2 * n].rearrange("p (e q) -> p e q", e=2)
                if own is not None:
                    pe.matmul(ps, kss[:, g, hp, own * P:(own + 1) * P], qss[:, g, hp, :, own * P:T], start=True, stop=False,
                              skip_group_check=True)
                    last = pe.matmul(ps[:, :, 0:P], ident16[:, :], mask_kq[:, :].unsqueeze(1).to_broadcast([P, 2, P]),
                                     start=False, stop=bool(c.cross), skip_group_check=True)
                    if not c.cross:
                        for e in range(2):
                            last = pe.matmul(ps[:, e, :], pick[:, hp, e, :], mrow[:, g % 2, own * P:T], start=False,
                                             stop=(e == 1), skip_group_check=True)
                else:
                    last = pe.matmul(ps, kst[:, g, hp, t * P:t * P + m], qst[:, g, hp, :, :], start=True, stop=True)
                last.then_inc(s.t_filled, 1)

            def pv_unit(b, g, u):
                pe.wait_ge(s.p_ready, lin(b, QUADS * c.NT, g * c.NT + 2 * u + 2))
                if u == 0:
                    pe.wait_ge(s.v_copied, lin(b, QUADS * c.nv, c.nv * (g + 1)))
                    if not (isinstance(b, int) and b == 0 and g == 0):
                        pe.wait_ge(s.o_evac, lin(b, QUADS, g))
                pr = p_ring[:, (g * c.NG + u) % 4]
                own, t, m, n = seg(c, u)
                for j in range(4):
                    if own is not None:
                        o0 = T * c.cross + own * P
                        last = pe.matmul(psum[32 * j:32 * j + VC, 6, o0:o0 + n], vs[:, g % 2, own, j, :], pr[:, j, 0:n],
                                         start=(own == 0), stop=(own == 1), skip_group_check=True)
                    else:
                        last = pe.matmul(psum[32 * j:32 * j + VC, 6, 0:T], vq[0:m, g % 2, t, j, :], pr[0:m, j, :],
                                         start=(t == 0), stop=(t == KT - 1), skip_group_check=True)
                last.then_inc(s.pv_done, 1)

            def emit(b, g, events=None):
                for ev in events or timeline(c, b, g):
                    kind = ev[0]
                    if kind == "T":
                        t_unit(b, g, ev[1], ev[2])
                    elif kind == "S":
                        b2, g2 = ahead(b, g, 2)
                        s_unit(b2, g2, ev[1], 0)
                    elif kind == "PV":
                        pv_unit(b, g, ev[1])
                    elif kind == "PVL":
                        b2, g2 = (b, g - 1) if g else (b - 1, 3)
                        pv_unit(b2, g2, c.NG - 1)
                    elif kind == "Mb":
                        m_turn(b, g, misc_index(b, g, "Mb"), *ahead(b, g, 1))
                    elif kind == "O":
                        i = misc_index(b, g, "O")
                        pe.wait_ge(s.misc_done, i)
                        pe.wait_ge(s.o_evac, lin(b, QUADS, g))
                        for k in range(2 * c.ns):
                            last = pe.transpose(misc_bank()[:, k * P:(k + 1) * P], osb[:, k * P:(k + 1) * P], ident[:, :])
                        last.then_inc(s.misc_filled, 1)
                    elif kind == "Y":
                        i = misc_index(b, g, "Y")
                        pe.wait_ge(s.misc_done, i)
                        pe.wait_ge(s.o_chain, lin(b, QUADS * c.O_OPS, g // 4 * QUADS * c.O_OPS))
                        for k in range(2):
                            last = pe.transpose(misc_bank()[:, k * P:(k + 1) * P], yb[:, k, :], ident[:, :])
                        last.then_inc(s.misc_filled, 1)
                    elif kind == "PR":
                        i = misc_index(b, g, "PR")
                        pe.wait_ge(s.misc_done, i)
                        for k in range(2):
                            last = pe.matmul(misc_bank()[:, k * C:(k + 1) * C], yT[:, k * P:(k + 1) * P], c.wo,
                                             start=True, stop=True)
                        last.then_inc(s.misc_filled, 1)

            def m_turn(b, g, i, bm, gm):
                if not (isinstance(i, int) and i == 0):
                    pe.wait_ge(s.misc_done, i)
                pe.wait_ge(s.m_chain, lin(bm, QUADS * c.M_OPS, c.M_OPS * (gm + 1)))
                mb = misc_bank().bitcast(BF16)
                n = 12 * c.ns
                for qt in range(2):
                    last = pe.transpose(mb[0:n, qt * P:(qt + 1) * P], mpt[:, qt * n:(qt + 1) * n], ident16[:, :])
                last.then_inc(s.misc_filled, 1)

            for k in range(c.NS):
                s_unit(0, 0, k, 0)
            m_turn(0, 0, 0, 0, 0)
            for k in range(c.NS):
                s_unit(0, 1, k, 0)
            steps(pe, emit)
            emit(B, 0, TAIL[:1])
            emit(B - 1, 4, TAIL[1:])

        def attn_act(act, c):
            s = c.at

            def emit(b, g, events=None):
                for ev in events or timeline(c, b, g):
                    if ev[0] == "T":
                        u, hp = ev[1], ev[2]
                        idx_c = g * c.NT + 2 * u + hp
                        grp = g * c.NG + u
                        act.wait_ge(s.t_filled, lin(b, QUADS * c.NT, idx_c + 1))
                        if hp == 0 and not (isinstance(b, int) and b == 0 and grp < 4):
                            act.wait_ge(s.pv_done, lin(b, QUADS * c.NG, grp - 3))
                        _, _, m, n = seg(c, u)
                        act.activation(p_ring[0:m, grp % 4, 2 * hp:2 * hp + 2, 0:n],
                                       psum[0:m, 4 + idx_c % 2, 0:2 * n].rearrange("p (e q) -> p e q", e=2), ACT.Exp,
                                       scale=SCALE).then_inc(s.p_ready, 1)
                    elif ev[0] == "OE":
                        act.wait_ge(s.pv_done, lin(b, QUADS * c.NG, g * c.NG))
                        if not (isinstance(b, int) and b == 0 and g <= 1):
                            bp, gp = (b, g - 1) if g else (b - 1, 3)
                            act.wait_ge(s.misc_filled, prev_o(bp, gp) + 1)
                        n = T * c.ns
                        act.activation(osb[:, 0:n], psum[:, 6, 0:n], ACT.Copy).then_inc(s.o_evac, 1)

            def prev_o(bp, gp):
                return misc_index(bp, gp, "O") if not (isinstance(bp, int) and bp == 0 and gp == 0) else 0

            steps(act, emit)
            act.wait_ge(s.pv_done, B * QUADS * c.NG)
            act.wait_ge(s.misc_filled, misc_index(B - 1, 3, "O") + 1)
            act.activation(osb[:, 0:T * c.ns], psum[:, 6, 0:T * c.ns], ACT.Copy).then_inc(s.o_evac, 1)

        def attn_dve(dve, c):
            s = c.at

            def s_max(b, g, k):
                idx_c = g * c.NS + k
                dve.wait_ge(s.s_filled, lin(b, QUADS * c.NS, idx_c + 1))
                bk = 2 * (idx_c % 2)
                if c.cross and k < 16:
                    j, qt, half = k // 4, k // 2 % 2, k % 2
                    je = (j % 2) * 2 + j // 2
                    dve.tensor_reduce(mp[:, g % 2, half, qt, je:je + 1], psum[:, bk:bk + 2, 0:SC], AX.XY, ALU.max)\
                       .then_inc(s.s_free, 1)
                else:
                    j = k - 16 * c.cross
                    je = (j % 2) * 2 + j // 2
                    dve.tensor_reduce(mps[:, g % 2, :, je], psum[:, bk, 0:3 * P].rearrange("p (a n) -> p a n", a=3),
                                      AX.X, ALU.max).then_inc(s.s_free, 1)

            def m_part(b, g, k):
                if k == 0:
                    dve.wait_ge(s.s_free, lin(b, QUADS * c.NS, (g + 1) * c.NS))
                else:
                    dve.wait_ge(s.m_chain, lin(b, QUADS * c.M_OPS, g * c.M_OPS + k))
                par, so = g % 2, c.ns - 1
                pt = mpt[:, 0:24 * c.ns].rearrange("p (q s e a h) -> p q s e a h", q=2, s=c.ns, e=2, a=3)

                def part(a):
                    return pt[:, :, :, :, a, :].rearrange("p q s e h -> p (q s e) h")

                what = (["halves"] * c.cross + ["first", "second"] * c.self_ + ["high", "rest", "middle", "low"])[k]
                if what == "halves":
                    ins = dve.tensor_tensor(mx[:, :, 0, :], mp[:, par, 0], mp[:, par, 1], ALU.max)
                elif what == "first":
                    ins = dve.tensor_copy(mx[:, 0, so, :], mps[:, par, 0, :])
                elif what == "second":
                    ins = dve.tensor_tensor(mx[:, 1, so, :], mps[:, par, 1, :], mps[:, par, 2, :], ALU.max)
                elif what == "high":
                    ins = dve.tensor_scalar(part(0), flat2(c, mx), -1.0, None, ALU.mult)
                elif what == "rest":
                    ins = dve.scalar_tensor_tensor(flat2(c, mr), flat2(c, mx), -1.0, part(0), ALU.mult, ALU.subtract)
                elif what == "middle":
                    ins = dve.tensor_copy(part(1), flat2(c, mr))
                else:
                    ins = dve.tensor_tensor(part(2), flat2(c, mr), part(1), ALU.subtract)
                ins.then_inc(s.m_chain, 1)

            def flat2(c, tile):
                if c.ns == 2:
                    return tile[:, :, :, :].rearrange("p q s (e h) -> p (q s e) h", e=2)
                return tile[:, :, 0, :].rearrange("p q (e h) -> p q e h", e=2)

            def m_rows(i, b, g):
                dve.wait_ge(s.misc_filled, i + 1)
                if not (isinstance(b, int) and b == 0 and g < 2):
                    b2, g2 = (b, g - 2) if g >= 2 else (b - 1, g + 2)
                    if c.cross:
                        dve.wait_ge(s.m_loaded[g2], lin(b2, 16 * c.nm, 16 * c.nm))
                    else:
                        dve.wait_ge(s.t_filled, lin(b2, QUADS * c.NT, (g2 + 1) * c.NT))
                n = 12 * c.ns
                dve.tensor_copy(mrow[0:n, g % 2, :], misc_bank().bitcast(BF16)[0:n, 0:T]).then_inc(s.misc_done, 1)

            def o_norm(i, b, g, gq, k):
                base = lin(b, QUADS * c.O_OPS, (g - 1) * c.O_OPS)
                bank = misc_bank()
                if k == 0:
                    dve.wait_ge(s.misc_filled, i + 1)
                    den = bank[:, 0:256 * c.ns].rearrange("p (n c) -> p n c", c=VC)[:, :, D]
                    dve.reciprocal(rec[:, 0:8 * c.ns], den).then_inc(s.o_chain, 1)
                elif k <= c.ns:
                    dve.wait_ge(s.o_chain, base + 1)
                    a = k - 1
                    num = bank[:, 256 * a:256 * (a + 1)].rearrange("p (q j c) -> p q j c", q=2, j=4)[:, :, :, 0:D]
                    r = rec[:, 8 * a:8 * a + 8].rearrange("p (q j) -> p q j", q=2).unsqueeze(3).to_broadcast([P, 2, 4, D])
                    dst = (yb, yb2)[a][:, :, 32 * gq:32 * gq + 32].rearrange("p q (j d) -> p q j d", j=4)
                    dve.tensor_tensor(dst, num, r, ALU.mult).then_inc(s.o_chain, 1)
                elif k < c.O_OPS:
                    dve.wait_ge(s.o_chain, base + 3)
                    ys = yb[:, :, 32 * gq:32 * gq + 32]
                    dve.tensor_tensor(ys, ys, yb2[:, :, 32 * gq:32 * gq + 32], ALU.add).then_inc(s.o_chain, 1)
                else:
                    dve.wait_ge(s.o_chain, base + c.O_OPS)
                    dve.sem_inc(s.misc_done, 1)

            def emit(b, g, events=None):
                for ev in events or timeline(c, b, g):
                    kind = ev[0]
                    if kind == "S":
                        s_max(*ahead(b, g, 2), ev[1])
                    elif kind == "Ma":
                        m_part(*ahead(b, g, 1), ev[1])
                    elif kind == "Mb":
                        m_rows(misc_index(b, g, "Mb"), *ahead(b, g, 1))
                    elif kind == "N":
                        o_norm(misc_index(b, g, "O"), b, g, (g - 1) % 4, ev[1])
                    elif kind == "Y":
                        dve.wait_ge(s.misc_filled, misc_index(b, g, "Y") + 1)
                        dve.tensor_copy(yT[:, :], misc_bank()[:, 0:T]).then_inc(s.misc_done, 1)
                    elif kind == "PR":
                        dve.wait_ge(s.misc_filled, misc_index(b, g, "PR") + 1)
                        xs = x[:, bass.ds((b - 1) * T, T)] if not isinstance(b, int) else x[:, (b - 1) * T:b * T]
                        dve.tensor_tensor(xs, misc_bank()[:, 0:T], xs, ALU.add).then_inc(s.misc_done, 1)

            for k in range(c.NS):
                s_max(0, 0, k)
            for k in range(c.M_OPS):
                m_part(0, 0, k)
            m_rows(0, 0, 0)
            for k in range(c.NS):
                s_max(0, 1, k)
            steps(dve, emit)
            for k in range(c.O_OPS + 1):
                o_norm(misc_index(B - 1, 4, "O"), B - 1, 4, 3, k)
            dve.wait_ge(s.misc_filled, misc_index(B - 1, 4, "Y") + 1)
            dve.tensor_copy(yT[:, :], misc_bank()[:, 0:T]).then_inc(s.misc_done, 1)
            dve.wait_ge(s.misc_filled, misc_index(B - 1, 4, "PR") + 1)
            xs = x[:, (B - 1) * T:B * T]
            dve.tensor_tensor(xs, misc_bank()[:, 0:T], xs, ALU.add).then_inc(s.misc_done, 1)

        def attn_pads(pool, c):
            def put(ins):
                count["made"] += 1
                ins.then_inc(made, 1)
                pool.wait_ge(made, count["made"])

            for tile in ([qst] if c.cross else []) + ([qss] if c.self_ else []):
                put(pool.memset(tile[:, :, :, :, :], 0.0))
            if c.name == "a":
                for tile in (kst, kss):
                    for e in range(2):
                        put(pool.memset(tile[64 * e + 32:64 * e + 64, :, :, :], 1.0))
                for tile in (vq, vs):
                    put(pool.memset(tile[:, :, :, :, :], 0.0))
                    for r in range(2):
                        put(pool.memset(tile[:, r, :, :, D:D + 1], 1.0))

        def attn_pool(pool, c):
            s = c.at

            def copies(b, g):
                r = g % 2
                if c.cross:
                    if g == 0:
                        pool_wait(pool, s.v_loaded, lin(b, 32, 32))
                    v = vb[:, :, 32 * g:32 * g + 32].rearrange("p t (j d) -> p t j d", j=4)
                    pool.tensor_copy(vq[:, r, 0:KT - 1, :, 0:D], v[:, 0:KT - 1]).then_inc(s.v_copied, 1)
                    pool.tensor_copy(vq[0:KLAST, r, KT - 1, :, 0:D], v[0:KLAST, KT - 1]).then_inc(s.v_copied, 1)
                if c.self_:
                    src = v_self[:, b * T:(b + 1) * T] if isinstance(b, int) else v_self[:, bass.ds(b * T, T)]
                    v = src.rearrange("p (k c) -> p k c", k=2)[:, :, 32 * g:32 * g + 32]\
                        .rearrange("p k (j d) -> p k j d", j=4)
                    pool.tensor_copy(vs[:, r, :, :, 0:D], v).then_inc(s.v_copied, 1)

            copies(0, 0)

            def emit(b, g):
                if isinstance(b, int) and b == B - 1 and g == 3:
                    return
                if not (isinstance(b, int) and b == 0 and g == 0):
                    pool_wait(pool, s.pv_done, lin(b, QUADS * c.NG, g * c.NG))
                copies(*ahead(b, g, 1))

            steps(pool, emit)

        def attn_sp(sp, c):
            s = c.at

            def col(b):
                return slice(b * T, (b + 1) * T) if isinstance(b, int) else bass.ds(b * T, T)

            def heads(g, e):
                return slice(4 * g + e, 4 * g + 4, 2)

            def quad_loads(b, g):
                q = s.kq_loaded[g]
                for e in range(2):
                    r0 = 64 * e
                    if c.cross:
                        kx = kx_d[b]
                        for t, n in ((0, 3), (3, 2), (5, 1)):
                            sp.dma_start(kst[r0 + D * t:r0 + D * (t + n), g, :, :],
                                         kx[heads(g, e), 0:n].rearrange("h p d n -> (p d) h n")).then_inc(q, 16)
                        sp.dma_start(qst[r0:r0 + ROWSM, g, :, e, :],
                                     qx_d[heads(g, e), :, col(b)].rearrange("h r n -> r h n")).then_inc(q, 16)
                    if c.self_:
                        sp.dma_start(qss[r0:r0 + ROWSM, g, :, e, :],
                                     qs_d[heads(g, e), :, col(b)].rearrange("h r n -> r h n")).then_inc(q, 16)
                        sp.dma_start(kss[r0:r0 + ROWS, g, :, :],
                                     ks_d[heads(g, e), :, col(b)].rearrange("h r n -> r h n")).then_inc(q, 16)

            def m_load(i, b, g):
                sp.wait_ge(s.misc_done, i + 1)
                for k in range(c.ns):
                    dst = (qst if c.cross and k == 0 else qss)
                    for e in range(2):
                        sp.dma_start(dst[64 * e + ROWS:64 * e + ROWSM, g, :, e, :],
                                     mrow[12 * k + 6 * e:12 * k + 6 * e + 6, g % 2, :]).then_inc(s.m_loaded[g], 16)

            def v_load(b):
                v = vx_d[b]
                full = (KT - 1) * P
                sp.dma_start(vb[:, 0:KT - 1, :], v[0:full].rearrange("(t p) c -> p t c", p=P)).then_inc(s.v_loaded, 16)
                sp.dma_start(vb[0:KLAST, KT - 1, :], v[full:TC]).then_inc(s.v_loaded, 16)

            if c.cross:
                v_load(0)
            for g in range(QUADS):
                quad_loads(0, g)
            if c.cross:
                m_load(0, 0, 0)

            def emit(b, g):
                last = isinstance(b, int) and b == B - 1
                if c.cross and not (last and g == 3):
                    m_load(misc_index(b, g, "Mb"), *ahead(b, g, 1))
                if last:
                    return
                sp.wait_ge(s.t_filled, lin(b, QUADS * c.NT, (g + 1) * c.NT))
                quad_loads(b + 1, g)
                if g == 2 and c.cross:
                    sp.wait_ge(s.v_copied, lin(b, QUADS * c.nv, QUADS * c.nv))
                    v_load(b + 1)

            steps(sp, emit)

        g_a = arenaB[:, 0:256].rearrange("p (t e) -> p t e", e=E)
        g_b = arenaB[:, 256:512].rearrange("p (t e) -> p t e", e=E)
        g_1 = arenaB[:, 512:768].rearrange("p (t e) -> p t e", e=E)
        g_2 = arenaB[:, 768:1024].rearrange("p (t e) -> p t e", e=E)
        g_c = arenaB[:, 1024:1280].rearrange("p (t e) -> p t e", e=E)
        g_s = arenaB[:, 1280:1312]
        g_m = arenaB[:, 1536:1792].rearrange("p (t e) -> p t e", e=E)
        gT = arenaB[0:E, 4096:8192]

        def bc(a):
            return a.unsqueeze(2).to_broadcast([P, TILES, E])

        def gate_sems(n):
            class r:
                dve, act, pe = sem(n + "_gt_dve"), sem(n + "_gt_act"), sem(n + "_gt_pe")
                b2, turned = sem(n + "_gt_b2"), sem(n + "_gt_turned")

            return r

        def gates_dve(dve, c):
            s = c.gt
            k = [0]

            def link(ins):
                k[0] += 1
                ins.then_inc(s.dve, 1)
                dve.wait_ge(s.dve, k[0])

            tt, L = dve.tensor_tensor, gate[:, :, :]
            link(dve.tensor_reduce(g_s, L, AX.X, ALU.max))
            link(tt(g_a, L, bc(g_s), ALU.subtract))
            dve.wait_ge(s.act, 1)
            link(dve.tensor_reduce(g_s, g_b, AX.X, ALU.add))
            link(dve.reciprocal(g_s, g_s))
            link(tt(L, g_b, bc(g_s), ALU.mult))
            for one, src in ((g_1, L), (g_2, g_a)):
                link(dve.tensor_reduce(g_s, src, AX.X, ALU.max))
                link(tt(g_b, src, bc(g_s), ALU.is_equal))
                link(tt(g_b, g_b, rank[:, :, :], ALU.mult))
                link(dve.tensor_reduce(g_s, g_b, AX.X, ALU.max))
                link(tt(one, g_b, bc(g_s), ALU.is_equal))
                if one is g_1:
                    link(dve.scalar_tensor_tensor(g_a, g_1, -2.0, L, ALU.mult, ALU.add))
            link(tt(g_m, g_1, g_2, ALU.add))
            link(tt(L, L, g_m, ALU.mult))
            c.mask_made = k[0]
            if c.capacity:
                dve.wait_ge(s.pe, 2)
                tot = psum[:, 1, 0:256].rearrange("p (t e) -> p t e", e=E)
                link(dve.memset(g_a, 0.0))
                link(dve.tensor_copy(g_a[:, 1:TILES, :], tot[:, 0:TILES - 1, :]))
                src, dst = g_a, g_b
                step = 1
                while step < TILES:
                    link(dve.tensor_copy(dst[:, 0:step, :], src[:, 0:step, :]))
                    link(tt(dst[:, step:, :], src[:, step:, :], src[:, 0:TILES - step, :], ALU.add))
                    src, dst = dst, src
                    step *= 2
                link(tt(g_c, psum[:, 0, 0:256].rearrange("p (t e) -> p t e", e=E), src, ALU.add))
                link(dve.tensor_scalar(g_c, g_c, float(CAP), None, ALU.is_le))
                link(tt(L, L, g_c, ALU.mult))
            c.gates_made = k[0]
            for ch in range(CHUNKS):
                dve.wait_ge(s.turned, ch + 1)
                dve.tensor_copy(gT[:, ch * 512:(ch + 1) * 512], psum[0:E, ch, :]).then_inc(s.b2, 1)
            for ch in range(CHUNKS):
                dve.wait_ge(s.turned, CHUNKS + ch + 1)
                xs = x[:, ch * 512:(ch + 1) * 512]
                dve.tensor_tensor(xs, psum[:, ch, :], xs, ALU.add).then_inc(s.b2, 1)

        def gates_act(act, c):
            act.wait_ge(c.gt.dve, 2)
            act.activation(g_b, g_a, ACT.Exp).then_inc(c.gt.act, 1)

        MASK_LINKS = 5 + 6 + 5 + 2

        def gates_pe(pe, c):
            s = c.gt
            pe.wait_ge(s.dve, MASK_LINKS)
            m = g_m.rearrange("p t e -> p (t e)")
            total = MASK_LINKS
            if c.capacity:
                pe.matmul(psum[:, 0, 0:256], upper[:, :], m, start=True, stop=True).then_inc(s.pe, 1)
                pe.matmul(psum[:, 1, 0:256], ones[:, :], m, start=True, stop=True).then_inc(s.pe, 1)
                total += 2 + 10 + 3
            pe.wait_ge(s.dve, total)
            for ch in range(CHUNKS):
                for t in range(4):
                    last = pe.transpose(psum[0:E, ch, t * P:(t + 1) * P], gate[:, 4 * ch + t, :], ident[:, :])
                last.then_inc(s.turned, 1)
            for ch in range(CHUNKS):
                pe.wait_ge(s.b2, ch + 1)
                for t in range(4):
                    last = pe.matmul(psum[:, ch, t * C:(t + 1) * C], gT[:, (4 * ch + t) * P:(4 * ch + t + 1) * P], b2s[:, :],
                                     start=True, stop=True)
                last.then_inc(s.turned, 1)

        w_in = arenaA[:, 0:4096].rearrange("p (e f) -> p e f", e=E)
        w_out = arenaA[:, 4096:8192].rearrange("p (e k c) -> p e k c", e=E, k=FC)
        w_up = arenaA[:, 8192:12288].rearrange("p (e f) -> p e f", e=E)
        f_y = [arenaB[:, 512 * i:512 * (i + 1)] for i in range(2)]
        f_h = [arenaB[:, 1024 + 512 * i:1024 + 512 * (i + 1)] for i in range(4)]
        NQ = E * FC

        def ffn_sems(n):
            class r:
                g, u, y, h, o = sem(n + "_g"), sem(n + "_u"), sem(n + "_y"), sem(n + "_h"), sem(n + "_o")
                acc, gch = sem(n + "_acc"), sem(n + "_gch")

            return r

        def chunks(eng, body):
            body(0, True)
            with eng.Fori(1, CHUNKS) as ch:
                body(ch, False)

        def cols(ch, off, n):
            return slice(ch * 512 + off, ch * 512 + off + n) if isinstance(ch, int) else bass.ds(ch * 512 + off, n)

        def ffn_pe(pe, c):
            s = c.ff

            def down(ch, first, q):
                e, k = q // FC, q % FC
                pe.wait_ge(s.h, nth(c, ch, NQ, q + 1))
                if k == 0 and not (first and e < 2):
                    pe.wait_ge(s.acc, nth(c, ch, E, e - 1))
                for t in range(4):
                    last = pe.matmul(psum[:, 4 + e % 2, t * C:(t + 1) * C], f_h[q % 4][:, t * P:(t + 1) * P],
                                     w_out[:, e, k, :], start=(k == 0 and t == 0), stop=(k == FC - 1),
                                     skip_group_check=True)
                last.then_inc(s.o, 1)

            def body(ch, first):
                src = xnT[:, cols(ch, 0, 512)]
                for q in range(NQ):
                    e, k = q // FC, q % FC
                    ready = s.y if c.gated else s.h
                    if not (first and q < 2):
                        pe.wait_ge(ready, nth(c, ch, NQ, q - 1))
                    pe.matmul(psum[:, q % 2, :], w_in[:, e, k * P:(k + 1) * P], src, start=True, stop=True).then_inc(s.g, 1)
                    if c.gated:
                        if not (first and q < 2):
                            pe.wait_ge(s.h, nth(c, ch, NQ, q - 1))
                        pe.matmul(psum[:, 2 + q % 2, :], w_up[:, e, k * P:(k + 1) * P], src, start=True, stop=True)\
                          .then_inc(s.u, 1)
                    if q:
                        down(ch, first, q - 1)
                down(ch, first, NQ - 1)

            chunks(pe, body)

        def ffn_act(act, c):
            s = c.ff

            def body(ch, first):
                for q in range(NQ):
                    e, k = q // FC, q % FC
                    act.wait_ge(s.g, nth(c, ch, NQ, q + 1))
                    if c.gated:
                        if not (first and q < 2):
                            act.wait_ge(s.h, nth(c, ch, NQ, q - 1))
                        act.activation(f_y[q % 2], psum[:, q % 2, :], ACT.Gelu, bias=b1s[:, 0, e, k:k + 1])\
                           .then_inc(s.y, 1)
                    else:
                        if not (first and q < 4):
                            act.wait_ge(s.o, nth(c, ch, NQ, q - 3))
                        act.activation(f_h[q % 4], psum[:, q % 2, :], ACT.Gelu, bias=b1s[:, 0, e, k:k + 1])\
                           .then_inc(s.h, 1)

            chunks(act, body)

        def ffn_dve(dve, c):
            s = c.ff

            def add_up(ch, e):
                dve.wait_ge(s.o, nth(c, ch, NQ, FC * (e + 1)))
                for t in range(4):
                    xs = x[:, cols(ch, t * P, P)]
                    last = dve.scalar_tensor_tensor(xs, psum[:, 4 + e % 2, t * C:(t + 1) * C], gch[:, t, e:e + 1], xs,
                                                    ALU.mult, ALU.add)
                last.then_inc(s.acc, 1)

            def body(ch, first):
                src = gate[:, :, :].rearrange("p t e -> p (t e)")
                gs = src[:, ch * 32:ch * 32 + 32] if isinstance(ch, int) else src[:, bass.ds(ch * 32, 32)]
                if not first:
                    dve.wait_ge(s.acc, nth(c, ch, E, 0))
                dve.tensor_copy(gch[:, :, :].rearrange("p t e -> p (t e)"), gs).then_inc(s.gch, 1)
                dve.wait_ge(s.gch, nth(c, ch, 1, 1))
                for q in range(NQ):
                    e, k = q // FC, q % FC
                    if c.gated:
                        dve.wait_ge(s.u, nth(c, ch, NQ, q + 1))
                        dve.wait_ge(s.y, nth(c, ch, NQ, q + 1))
                        if not (first and q < 4):
                            dve.wait_ge(s.o, nth(c, ch, NQ, q - 3))
                        dve.scalar_tensor_tensor(f_h[q % 4], psum[:, 2 + q % 2, :], b1s[:, 1, e, k:k + 1], f_y[q % 2],
                                                 ALU.add, ALU.mult).then_inc(s.h, 1)
                    if k == 1 and e:
                        if e > 1 or not first:
                            dve.wait_ge(s.acc, nth(c, ch, E, e - 1))
                        add_up(ch, e - 1)
                dve.wait_ge(s.acc, nth(c, ch, E, E - 1))
                add_up(ch, E - 1)

            chunks(dve, body)

        def W(i):
            return wbig[:, i, :]

        c1 = Part(cross=1, self_=1, affine=False, vbias=True, projs="QQQV", weights=[(W(0),), (W(1),), (W(2),), (W(3),)],
                             stores=[(qs_d, TERMS_Q), (ks_d, TERMS_K), (qx_d, TERMS_Q)], wo=W(5), resid_bias=True)
        c2 = Part(affine=False, projs="G", weights=[(rw[:, :],)], stores=[], gated=True, capacity=False, resid_bias=False)
        c3 = Part(cross=1, self_=0, affine=False, vbias=False, projs="Q", weights=[(W(0),)],
                             stores=[(qx_d, TERMS_Q)], wo=W(5), resid_bias=True)
        c4 = Part(cross=0, self_=1, affine=True, vbias=False, projs="RRV",
                             weights=[(W(0), W(1)), (W(2), W(3)), (W(4),)],
                             stores=[(qs_d, TERMS_Q), (ks_d, TERMS_K)], wo=W(5), resid_bias=False)
        c5 = Part(affine=True, projs="G", weights=[(rw[:, :],)], stores=[], gated=False, capacity=True, resid_bias=False)
        parts = [("a", c1), ("b", c2), ("c", c3), ("d", c4), ("e", c5)]
        cx_s, ff_s, biased = ctx_sems("cx"), ffn_sems("ff"), sem("biased")
        for n, c in parts:
            c.name = n
            c.items = proj_plan(c)
            c.nth = {"a": 0, "b": 1, "c": 2, "d": 4, "e": 5}[n]
            c.pj = proj_sems(n, c)
            c.attn = n in "acd"
            c.stop = False
            if c.attn:
                if c.cross:
                    c.cx = cx_s
                    c.turn = n == "c"
                attn_cfg(c, n)
            else:
                c.gt = gate_sems(n)
                c.ff = ff_s
                c.turn = n == "e"
            c.biased = biased

        def copy_in(sp, pairs_):
            for dst, src in pairs_:
                sp.dma_start(dst, src).then_inc(loaded, 16)
                count["in"] = count.get("in", 0) + 16
            sp.wait_ge(loaded, count["in"])

        def part_inputs(n):
            if n == "a":
                return ([(W(i), A["w_a"][i]) for i in range(6)] +
                        [(colv[:, i:i + 1], A["col_a"][i]) for i in range(3)] +
                        [(rowv[:, 0, :], A["bp"]), (rowv[:, 1, :], A["bv"]), (wkv[0:CC + 1, 0, :], A["wk_a"]), (wkv[0:CC + 1, 1, :], A["wv_a"])])
            if n == "b":
                return [(rw[:, :], A["rw_b"]), (w_in.rearrange("p e f -> p (e f)"), A["wg_b"]),
                        (w_up.rearrange("p e f -> p (e f)"), A["w1_b"]), (w_out.rearrange("p e k c -> p (e k c)"), A["w2_b"]),
                        (b1s[:, 0], A["bg_b"]), (b1s[:, 1], A["b1_b"]), (b2s[:, :], A["b2_b"])]
            if n == "c":
                return [(W(0), A["w_c"][0]), (W(5), A["w_c"][1]), (colv[:, 0:1], A["col_c"]), (rowv[:, 0, :], A["bo"]),
                        (wkv[0:CC + 1, 0, :], A["wk_c"]), (wkv[0:CC + 1, 1, :], A["wv_c"])]
            if n == "d":
                return [(W(i), A["w_d"][i]) for i in range(6)] + [(colv[:, 2:3], A["ln1g"]), (colv[:, 3:4], A["ln1b"]),
                                                              (rope[:, :, :], A["rope"])]
            return [(rw[:, :], A["rw_e"]), (w_in.rearrange("p e f -> p (e f)"), A["w1_e"]),
                    (w_out.rearrange("p e k c -> p (e k c)"), A["w2_e"]), (b1s[:, 0], A["b1_e"]), (b2s[:, :], A["b2_e"]),
                    (colv[:, 2:3], A["ln2g"]), (colv[:, 3:4], A["ln2b"]), (res, res_d.rearrange("p t c -> p (t c)"))]

        block = ctx.enter_context(nc.Block())
        x_dram = A["x"].rearrange("b (q p) c -> p (b q) c", p=P)
        out_dram = out.rearrange("b (q p) c -> p (b q) c", p=P)

        @block.sync
        def _(sp):
            copy_in(sp, [(x3, x_dram)])
            sp.wait_ge(made, 1)
            zero = arenaA[0:3 * H, 0:TOK // 2].bitcast(BF16)
            copy_in(sp, [(d[:, ROWS:ROWSM, :], zero) for d in (qx_d, qs_d)])
            phase_end(sp, "sp")
            for n, c in parts:
                if n == "d":
                    copy_in(sp, [(res_d, x3)])
                    phase_end(sp, "sp")
                    phase_end(sp, "sp")
                copy_in(sp, part_inputs(n))
                phase_end(sp, "sp")
                proj_sp(sp, c)
                phase_end(sp, "sp")
                if c.attn and c.cross:
                    ctx_sp(sp, c)
                    phase_end(sp, "sp")
                if c.attn:
                    attn_sp(sp, c)
                    phase_end(sp, "sp")
                else:
                    phase_end(sp, "sp")
                    phase_end(sp, "sp")
            sp.dma_start(out_dram, x3).then_inc(loaded, 16)
            sp.wait_ge(loaded, count["in"] + 16)

        @block.gpsimd
        def _(pool):
            k = [0]

            def link(ins):
                k[0] += 1
                ins.then_inc(made, 1)
                pool.wait_ge(made, k[0])

            big = arenaB[:, 0:P]
            link(pool.memset(arenaA[0:3 * H, 0:TOK // 2], 0.0))
            link(pool.memset(eps_col[:, :], EPS))
            link(pool.memset(ones[:, :], 1.0))
            link(pool.memset(ident[:, :], 0.0))
            link(pool.affine_select(out=ident[:, :], in_=ident[:, :], compare_op=ALU.not_equal, fill=1.0, base=0,
                                    pattern=[[-1, P]], channel_multiplier=1))
            link(pool.tensor_copy(ident16[:, :], ident[:, :]))
            link(pool.affine_select(out=upper[:, :], in_=ones[:, :], compare_op=ALU.is_ge, fill=0.0, base=0,
                                    pattern=[[1, P]], channel_multiplier=-1))
            link(pool.memset(big, 0.0))
            link(pool.affine_select(out=big, in_=big, compare_op=ALU.is_ge, fill=MASKED, base=0,
                                    pattern=[[-1, P]], channel_multiplier=1))
            link(pool.tensor_copy(mask_qk[:, :], big))
            link(pool.memset(big, 0.0))
            link(pool.affine_select(out=big, in_=big, compare_op=ALU.is_ge, fill=MASKED, base=0,
                                    pattern=[[1, P]], channel_multiplier=-1))
            link(pool.tensor_copy(mask_kq[:, :], big))
            link(pool.memset(mrow[:, :, :], 0.0))
            for hp in range(2):
                for e in range(2):
                    one, r = big[:, 2 * hp + e:2 * hp + e + 1], 6 * e + hp
                    link(pool.tensor_tensor(one, ident[:, r:r + 1], ident[:, r + 2:r + 3], ALU.add))
                    link(pool.tensor_tensor(one, one, ident[:, r + 4:r + 5], ALU.add))
                    link(pool.tensor_copy(pick[:, hp, e, :], one.to_broadcast([P, P])))
            link(pool.memset(wkv[:, :, :], 0.0))
            for e in range(E):
                link(pool.memset(rank[:, :, e:e + 1], float(E - e)))
            count["made"] = k[0]
            phase_end(pool, "pool")
            for n, c in parts:
                if n == "d":
                    phase_end(pool, "pool")
                    phase_end(pool, "pool")
                if c.attn:
                    attn_pads(pool, c)
                phase_end(pool, "pool")
                if n == "e":
                    pool.tensor_tensor(x[:, :], x[:, :], res, ALU.add).then_inc(biased, 1)
                if c.resid_bias:
                    pool.tensor_tensor(x3, x3, rowv[:, 0, :].unsqueeze(1).to_broadcast([P, TILES, C]), ALU.add)\
                        .then_inc(c.biased, 1)
                proj_pool(pool, c)
                phase_end(pool, "pool")
                if c.attn and c.cross:
                    ctx_pool(pool, c)
                    phase_end(pool, "pool")
                if c.attn:
                    attn_pool(pool, c)
                    phase_end(pool, "pool")
                else:
                    phase_end(pool, "pool")
                    phase_end(pool, "pool")

        @block.scalar
        def _(act):
            phase_end(act, "act")
            for n, c in parts:
                if n == "d":
                    ln_act(act, 3)
                    phase_end(act, "act")
                    act.activation(x[:, 0:TOK // 2], xn[:, 0:TOK // 2], ACT.Copy)
                    phase_end(act, "act")
                ln_act(act, c.nth)
                phase_end(act, "act")
                proj_act(act, c)
                phase_end(act, "act")
                if c.attn and c.cross:
                    ctx_act(act, c)
                    phase_end(act, "act")
                if c.attn:
                    attn_act(act, c)
                    phase_end(act, "act")
                else:
                    gates_act(act, c)
                    phase_end(act, "act")
                    ffn_act(act, c)
                    phase_end(act, "act")

        @block.vector
        def _(dve):
            phase_end(dve, "dve")
            for n, c in parts:
                if n == "d":
                    ln_dve(dve, 3)
                    phase_end(dve, "dve")
                    dve.tensor_copy(x[:, TOK // 2:TOK], xn[:, TOK // 2:TOK])
                    phase_end(dve, "dve")
                ln_dve(dve, c.nth)
                phase_end(dve, "dve")
                proj_dve(dve, c)
                phase_end(dve, "dve")
                if c.attn and c.cross:
                    ctx_dve(dve, c)
                    phase_end(dve, "dve")
                if c.attn:
                    attn_dve(dve, c)
                    phase_end(dve, "dve")
                else:
                    gates_dve(dve, c)
                    phase_end(dve, "dve")
                    ffn_dve(dve, c)
                    phase_end(dve, "dve")

        @block.tensor
        def _(pe):
            phase_end(pe, "pe")
            for n, c in parts:
                if n == "d":
                    phase_end(pe, "pe")
                    phase_end(pe, "pe")
                phase_end(pe, "pe")
                proj_pe(pe, c)
                phase_end(pe, "pe")
                if c.attn and c.cross:
                    ctx_pe(pe, c)
                    phase_end(pe, "pe")
                if c.attn:
                    attn_pe(pe, c)
                    phase_end(pe, "pe")
                else:
                    gates_pe(pe, c)
                    phase_end(pe, "pe")
                    ffn_pe(pe, c)
                    phase_end(pe, "pe")


def lay_out(i):
    import numpy as np
    i = {k: np.asarray(v) for k, v in i.items()}
    col = lambda a: np.ascontiguousarray(a.reshape(C, 1))
    rows = lambda a: np.ascontiguousarray(np.broadcast_to(a, (P, C)))
    withb = lambda w, b: np.concatenate([w, b[None, :]], 0)
    L = "L0_xattn_"
    a = {"x": i["x"], "ctxT": np.ascontiguousarray(i["ctx_512"].transpose(0, 2, 1))}
    a["w_a"] = np.stack([i[L + "Wq"], i[L + "Wk"], i[L + "Wcq"], i[L + "Wv"], i[L + "Wp"], i[L + "Wp"]])
    a["col_a"] = np.stack([col(i[L + n]) for n in ("bq", "bk", "bcq")])
    a["bp"], a["bv"] = rows(i[L + "bp"]), rows(i[L + "bv"])
    a["wk_a"], a["wv_a"] = withb(i[L + "Wck"], i[L + "bck"]), withb(i[L + "Wcv"], i[L + "bcv"])
    L = "L0_ffn_"
    a["rw_b"] = np.ascontiguousarray(i[L + "router_w"].T)
    inw = lambda w: np.ascontiguousarray(w.transpose(2, 0, 1).reshape(C, E * F))
    a["wg_b"], a["w1_b"] = inw(i[L + "wg_w"]), inw(i[L + "w1_w"])
    a["w2_b"] = np.ascontiguousarray(i[L + "w2_w"].reshape(E, C, FC, P).transpose(3, 0, 2, 1).reshape(P, E * FC * C))
    bias = lambda b: np.ascontiguousarray(b.reshape(E, FC, P).transpose(2, 0, 1))
    a["bg_b"], a["b1_b"], a["b2_b"] = bias(i[L + "wg_b"]), bias(i[L + "w1_b"]), i[L + "w2_b"]
    L = "L1_xattn_"
    a["w_c"] = np.stack([i[L + "Wq"], i[L + "Wo"]])
    a["col_c"], a["bo"] = col(i[L + "bq"]), rows(i[L + "bo"])
    a["wk_c"], a["wv_c"] = withb(i[L + "Wk"], i[L + "bk"]), withb(i[L + "Wv"], i[L + "bv"])
    L = "L1_ffn_"
    w = i[L + "Wqkv"].reshape(C, H, 3, D)
    wq, wk, wv = (np.ascontiguousarray(w[:, :, n, :]).reshape(C, C) for n in range(3))
    half = D // 2
    turn = np.array([h * D + (d + half) % D for h in range(H) for d in range(D)])
    a["w_d"] = np.stack([wq, wq[:, turn], wk, wk[:, turn], wv, i[L + "Wproj"]])
    inv = (1.0 / 10000.0 ** (np.arange(0, D, 2, dtype=np.float32) / D)).astype(np.float32)
    ang = np.arange(T, dtype=np.float32)[:, None] * inv
    cos, sin = np.cos(ang).T, np.sin(ang).T
    a["rope"] = np.stack([np.tile(np.concatenate([cos, cos]), (H, 1)),
                          np.tile(np.concatenate([-sin, sin]), (H, 1))], 1).astype(np.float32)
    a["ln1g"], a["ln1b"] = col(i[L + "ln1_g"]), col(i[L + "ln1_b"])
    a["ln2g"], a["ln2b"] = col(i[L + "ln2_g"]), col(i[L + "ln2_b"])
    a["rw_e"] = i[L + "Wgate"]
    a["w1_e"] = np.ascontiguousarray(i[L + "W1"].transpose(1, 0, 2).reshape(C, E * F))
    a["w2_e"] = np.ascontiguousarray(i[L + "W2"].reshape(E, FC, P, C).transpose(2, 0, 1, 3).reshape(P, E * FC * C))
    a["b1_e"], a["b2_e"] = bias(i[L + "b1"]), i[L + "b2"]
    return {k: np.ascontiguousarray(v) for k, v in a.items()}


def kernel(**inputs):
    import concourse.bacc as bacc
    from concourse.bass_utils import run_bass_kernel_spmd

    arrays = lay_out(inputs)
    nc = bacc.Bacc("TRN2", target_bir_lowering=False, num_devices=1)
    aps = {k: nc.dram_tensor(f"in_{k}", v.shape, mybir.dt.from_np(v.dtype), kind="ExternalInput").ap()
           for k, v in arrays.items()}
    out = nc.dram_tensor("out_x", (B, T, C), F32, kind="ExternalOutput").ap()
    build(nc, aps, out)
    r = run_bass_kernel_spmd(nc, [{f"in_{k}": v for k, v in arrays.items()}], core_ids=[0])
    return r.results[0]["out_x"]
```

```python
from contextlib import ExitStack

import concourse.bass as bass
from concourse import mybir

F32 = mybir.dt.float32
BF16 = mybir.dt.bfloat16
F32R = mybir.dt.float32r
ALU = mybir.AluOpType
ACT = mybir.ActivationFunctionType
AX = mybir.AxisListType


class Item:

    def __init__(self, kind, ch, p, banks, frees):
        self.kind, self.ch, self.p, self.banks, self.frees = kind, ch, p, banks, frees


class Part:

    def __init__(self, cross=0, self_=0, affine=False, vbias=False, projs="", weights=(), stores=(), wo=None,
                 resid_bias=False, gated=False, capacity=False):
        self.cross, self.self_, self.affine, self.vbias = cross, self_, affine, vbias
        self.projs, self.weights, self.stores, self.wo = projs, weights, stores, wo
        self.resid_bias, self.gated, self.capacity = resid_bias, gated, capacity


P = 128
B = 16
T = 256
C = 128
TILES = B * T // P
TOK = B * T
H = 16
D = C // H
TC = 1601
CC = 64
SCALE = float(D) ** -0.5
KT = (TC + P - 1) // P
KLAST = TC - (KT - 1) * P
QUADS = H // 4
TERMS_Q = (0, 0, 0, 1, 1, 2)
TERMS_K = (0, 1, 2, 0, 1, 0)
ROWS = 6 * D
ROWSM = ROWS + 3
SC = 401
SSTART = (0, SC, 2 * SC, TC - SC)
VC = 32
E = 8
F = 512
FC = F // P
CAP = 1024
EPS = 1e-5
MASKED = -1.0e30
CHUNKS = TOK // 512
KCH = ((0, 401), (401, 401), (802, 401), (1203, 398))


def lin(b, per, c):
    return b * per + c


def build(nc, A, out):
    ctx = ExitStack()
    with ctx:
        def sb(name, shape, dt=F32):
            return ctx.enter_context(nc.sbuf_tensor(name, shape, dt))

        def sem(name):
            if name not in sems:
                sems[name] = ctx.enter_context(nc.semaphore(name))
            return sems[name]

        sems = {}

        def scratch(name, shape, dt):
            return nc.dram_tensor(name, shape, dt).ap()

        x = sb("x", [P, TOK])
        xnT = sb("xnT", [P, TOK])
        arenaA = sb("arenaA", [P, 12288])
        arenaB = sb("arenaB", [P, 12992])
        ident = sb("ident", [P, P])
        ident16 = sb("ident16", [P, P], BF16)
        mask_qk = sb("mask_qk", [P, P], BF16)
        mask_kq = sb("mask_kq", [P, P], BF16)
        upper = sb("upper", [P, P])
        ones = sb("ones", [P, P])
        rank = sb("rank", [P, TILES, E])
        stat = sb("stat", [P, 4, TILES])
        kst = sb("kst", [P, QUADS, 2, TC], BF16)
        kss = sb("kss", [P, QUADS, 2, T], BF16)
        xh, xl = sb("xh", [P, 2, 512], F32R), sb("xl", [P, 2, 512], F32R)
        wh, wl = sb("wh", [P, FC, 2, P], F32R), sb("wl", [P, FC, 2, P], F32R)
        osb = sb("osb", [P, 2 * T])
        rec = sb("rec", [P, 16])
        mp = sb("mp", [P, 2, 2, 2, 4])
        mps = sb("mps", [P, 2, 3, 4])
        mx = sb("mx", [P, 2, 2, 4])
        mr = sb("mr", [P, 2, 2, 4])
        mpt = sb("mpt", [P, 48], BF16)
        mrow = sb("mrow", [P, 2, T], BF16)
        pick = sb("pick", [P, 2, 2, P], BF16)
        wbig = sb("wbig", [P, 6, C])
        wkv = sb("wkv", [P, 2, C])
        colv = sb("colv", [P, 4])
        rowv = sb("rowv", [P, 2, C])
        rope = sb("rope", [P, 2, T])
        b1s = sb("b1s", [P, 2, E, FC])
        b2s = sb("b2s", [E, C])
        rw = sb("rw", [P, E])
        gate = osb[:, 0:TILES * E].rearrange("p (t e) -> p t e", e=E)
        gch = osb[:, TILES * E:TILES * E + 4 * E].rearrange("p (t e) -> p t e", e=E)

        psum = ctx.enter_context(nc.psum_tensor("psum", [P, 8, 512], F32))

        p_ring = arenaA[:, 0:4096].rearrange("p (s j n) -> p s j n", s=4, j=4)
        v_self = arenaA[:, 8192:12288]
        qst, qss = (arenaA[:, lo:lo + 2048].bitcast(BF16).rearrange("p (g j e n) -> p g j e n", g=QUADS, j=2, e=2)
                    for lo in (4096, 6144))
        vq = arenaB[:, 0:3328].rearrange("p (r t j c) -> p r t j c", r=2, t=KT, j=4)
        vs = arenaB[:, 3328:3840].rearrange("p (r t j c) -> p r t j c", r=2, t=2, j=4)
        vb = arenaB[:, 3840:5504].rearrange("p (t c) -> p t c", t=KT)
        yb, yb2 = (arenaB[:, lo:lo + 2 * C].rearrange("p (k c) -> p k c", k=2) for lo in (5504, 5760))
        yT = arenaB[:, 6016:6272]
        xn = arenaB[:, 0:4096]
        q_parts = [arenaB[:, 4096 + 1536 * i:4096 + 1536 * (i + 1)].bitcast(BF16).rearrange("p (a n) -> p a n", a=3)
                   for i in range(3)]
        q_res = [arenaB[:, 8704 + 512 * i:8704 + 512 * (i + 1)] for i in range(4)]
        q_x32 = [arenaB[:, 10752 + 512 * i:10752 + 512 * (i + 1)] for i in range(2)]
        q_t1 = arenaB[:, 11776:12288]
        q_t2 = arenaB[:, 12288:12800]
        cx = [arenaB[:, TC * i:TC * (i + 1)] for i in range(2)]
        at = 2 * TC
        k_res = [arenaB[:, at + SC * i:at + SC * (i + 1)] for i in range(4)]
        at += 4 * SC
        k_parts = [arenaB[:, at + 2402 * i:at + 2402 * (i + 1)].bitcast(BF16)[:, 0:3 * TC].rearrange(
            "p (a n) -> p a n", a=3) for i in range(2)]
        at += 2 * 2402
        v_st = [arenaB[:, at + KT * C * i:at + KT * C * (i + 1)].rearrange("p (t c) -> p t c", t=KT) for i in range(2)]
        at += 2 * KT * C
        assert at <= 12992

        kx_d = scratch("kx_d", [B, H, 3, D, TC], BF16)
        vx_d = scratch("vx_d", [B, TC, C], F32)
        qx_d = scratch("qx_d", [H, ROWSM, TOK], BF16)
        qs_d = scratch("qs_d", [H, ROWSM, TOK], BF16)
        ks_d = scratch("ks_d", [H, ROWS, TOK], BF16)
        res_d = scratch("res_d", [P, TILES, C], F32)
        res = arenaB[:, 8192:12288]

        phase_done = sem("phase_done")
        loaded = sem("loaded")
        made = sem("made")

        count = {}

        waited = sem("waited")

        def pool_wait(pool, sm, value):
            pool.wait_ge(sm, value)
            if not isinstance(value, int):
                pool.sem_inc(waited, 1)

        def phase_end(eng, name):
            count[name] = count.get(name, 0) + 1
            eng.drain().then_inc(phase_done, 1)
            eng.wait_ge(phase_done, 5 * count[name])

        class ln_s:
            dve, act = sem("ln_dve"), sem("ln_act")

        CENTRED, SUMMED, SCALED = (3, 6, 12, 18), (7, 13, 19, 22), (9, 15, 21, 24)
        SQUARED, ROOT = (1, 2, 4, 6), (3, 5, 7, 8)
        LN_STAGES = ((("c", 0), ("c", 1), ("s", 0), ("c", 2), ("s", 1)), (("c", 3), ("s", 2)), (("s", 3),), ())

        x3 = x[:, :].rearrange("p (t c) -> p t c", c=C)
        xn3 = xn.rearrange("p (t c) -> p t c", c=C)
        sq3 = xnT[:, :].rearrange("p (t c) -> p t c", c=C)

        def ln_dve(dve, k, j):
            s, base = ln_s, 24 * k
            for stage, q in LN_STAGES[j]:
                ts = slice(8 * q, 8 * q + 8)
                over = lambda a: stat[:, a, ts].unsqueeze(2).to_broadcast([P, 8, C])
                if stage == "c":
                    n = base + CENTRED[q]
                    dve.tensor_reduce(stat[:, 0, ts], x3[:, ts, :], AX.X, ALU.add).then_inc(s.dve, 1)
                    dve.wait_ge(s.dve, n - 2)
                    dve.tensor_scalar(stat[:, 1, ts], stat[:, 0, ts], 1.0 / C, None, ALU.mult).then_inc(s.dve, 1)
                    dve.wait_ge(s.dve, n - 1)
                    dve.tensor_tensor(xn3[:, ts, :], x3[:, ts, :], over(1), ALU.subtract).then_inc(s.dve, 1)
                else:
                    dve.wait_ge(s.act, 8 * k + SQUARED[q])
                    dve.tensor_reduce(stat[:, 2, ts], sq3[:, ts, :], AX.X, ALU.add).then_inc(s.dve, 1)
                    dve.wait_ge(s.act, 8 * k + ROOT[q])
                    dve.reciprocal(stat[:, 1, ts], stat[:, 3, ts]).then_inc(s.dve, 1)
                    dve.wait_ge(s.dve, base + SCALED[q] - 1)
                    dve.tensor_tensor(xn3[:, ts, :], xn3[:, ts, :], over(1), ALU.mult).then_inc(s.dve, 1)

        def ln_act(act, k, j):
            s = ln_s
            for stage, q in LN_STAGES[j]:
                ts, cs = slice(8 * q, 8 * q + 8), slice(1024 * q, 1024 * (q + 1))
                if stage == "c":
                    act.wait_ge(s.dve, 24 * k + CENTRED[q])
                    act.activation(xnT[:, cs], xn[:, cs], ACT.Square).then_inc(s.act, 1)
                else:
                    act.wait_ge(s.dve, 24 * k + SUMMED[q])
                    act.activation(stat[:, 3, ts], stat[:, 2, ts], ACT.Sqrt, bias=eps_col[:, 0:1], scale=1.0 / C)\
                       .then_inc(s.act, 1)

        eps_col = sb("eps_col", [P, 1])

        def proj_plan(c):
            order = [("T", 0), ("T", 1)]
            for ch in range(0, CHUNKS, 2):
                if ch + 2 < CHUNKS:
                    order += [("T", ch + 2), ("T", ch + 3)]
                order += [(kind, ch + k, p) for p, kind in enumerate(c.projs) for k in range(2)]
            items, bank, owner = [], 0, [None] * 8
            nact = ndve = nq = 0
            for it in order:
                kind = it[0]
                n = 2 if kind == "R" else 1
                if n == 2 and bank % 2:
                    bank += 1
                banks = [(bank + k) % 8 for k in range(n)]
                bank += n
                o = Item(kind=kind, ch=it[1], p=it[2] if len(it) > 2 else None, banks=banks,
                                    frees=[owner[k] for k in banks if owner[k]])
                if kind == "T":
                    nact += 1
                    mine = ("act", nact)
                else:
                    ndve += 1
                    mine = ("dve", ndve)
                    if kind in "QR":
                        o.q = nq
                        nq += 1
                for k in banks:
                    owner[k] = mine
                o.freed = mine[1]
                items.append(o)
            return items

        def proj_sems(n, c):
            class r:
                filled, act, dve = sem(n + "_pj_filled"), sem(n + "_pj_act"), sem(n + "_pj_dve")

            if c.stores:
                r.mid, r.low = sem(n + "_pj_mid"), sem(n + "_pj_low")
                r.stored = [sem(f"{n}_pj_stored{i}") for i in range(3)]
                if "R" in c.projs:
                    r.rp = sem(n + "_pj_rope")
                else:
                    r.high = sem(n + "_pj_high")
            return r

        def proj_pe(pe, c):
            for i, o in enumerate(c.items):
                if i == 2:
                    pe.wait_ge(loaded, c.loaded)
                if o.kind == "T":
                    pe.wait_ge(ln_s.dve, 24 * c.nth + SCALED[o.ch // 2])
                for who, v in o.frees:
                    pe.wait_ge(c.pj.act if who == "act" else c.pj.dve, v)
                bk = psum[:, o.banks[0], :]
                if o.kind == "T":
                    for t in range(4):
                        k = 4 * o.ch + t
                        last = pe.transpose(bk[:, t * P:(t + 1) * P], xn[:, k * P:(k + 1) * P], ident[:, :])
                else:
                    pe.wait_ge(c.pj.act, o.ch + 1)
                    src = xnT[:, o.ch * 512:(o.ch + 1) * 512]
                    w = c.weights[o.p]
                    if o.kind == "Q":
                        last = pe.matmul(bk, w[0], src, start=True, stop=True)
                    elif o.kind == "R":
                        pe.matmul(bk, w[0], src, start=True, stop=True)
                        last = pe.matmul(psum[:, o.banks[1], :], w[1], src, start=True, stop=True)
                    else:
                        n = C if o.kind == "V" else E
                        for t in range(4):
                            last = pe.matmul(bk[:, t * n:(t + 1) * n], src[:, t * P:(t + 1) * P], w[0],
                                             start=True, stop=True)
                last.then_inc(c.pj.filled, 1)

        def proj_act(act, c):
            pending = []

            def middle(o):
                act.wait_ge(c.pj.dve, o.freed)
                act.activation(q_part(o, 1), q_res[o.q % 4], ACT.Copy).then_inc(c.pj.mid, 1)

            for i, o in enumerate(c.items):
                bk = psum[:, o.banks[0], :]
                if o.kind == "T" and o.ch % 2 == 0:
                    ln_act(act, c.nth, o.ch // 2)
                    if i == 0:
                        act.wait_ge(loaded, c.loaded)
                if o.kind == "T":
                    act.wait_ge(c.pj.filled, i + 1)
                    dst = xnT[:, o.ch * 512:(o.ch + 1) * 512]
                    if c.affine:
                        act.activation(dst, bk, ACT.Identity, bias=colv[:, 3:4], scale=colv[:, 2:3]).then_inc(c.pj.act, 1)
                    else:
                        act.activation(dst, bk, ACT.Copy).then_inc(c.pj.act, 1)
                elif o.kind == "Q":
                    act.wait_ge(c.pj.filled, i + 1)
                    stores_wait(act, c, o)
                    act.activation(q_part(o, 0), bk, ACT.Identity,
                                   bias=colv[:, o.p:o.p + 1]).then_inc(c.pj.high, 1)
                if o.kind in "QR":
                    pending.append(o)
                    if len(pending) > 1:
                        middle(pending.pop(0))
            for o in pending:
                middle(o)

        def proj_dve(dve, c):
            rp = 0
            pending = []

            def low(o):
                dve.wait_ge(c.pj.mid, o.q + 1)
                dve.tensor_tensor(q_part(o, 2), q_res[o.q % 4], q_part(o, 1),
                                  ALU.subtract).then_inc(c.pj.low, 1)

            for i, o in enumerate(c.items):
                if o.kind == "T":
                    if o.ch % 2 == 0:
                        ln_dve(dve, c.nth, o.ch // 2)
                    if i == 0:
                        dve.wait_ge(loaded, c.loaded)
                    continue
                bk = psum[:, o.banks[0], :]
                dve.wait_ge(c.pj.filled, i + 1)
                if o.kind == "Q":
                    dve.wait_ge(c.pj.high, o.q + 1)
                    if o.q >= 4:
                        dve.wait_ge(c.pj.low, o.q - 3)
                    dve.scalar_tensor_tensor(q_res[o.q % 4], bk, colv[:, o.p:o.p + 1], q_part(o, 0),
                                             ALU.add, ALU.subtract).then_inc(c.pj.dve, 1)
                    pending.append(o)
                elif o.kind == "R":
                    view = lambda a: a.rearrange("p (b t) -> p b t", b=2)
                    tab = lambda k: rope[:, k, :].unsqueeze(1).to_broadcast([P, 2, T])
                    x32 = q_x32[o.q % 2]
                    dve.wait_ge(c.pj.rp, rp)
                    dve.tensor_tensor(view(q_t1), view(bk), tab(0), ALU.mult).then_inc(c.pj.rp, 1)
                    dve.tensor_tensor(view(q_t2), view(psum[:, o.banks[1], :]), tab(1), ALU.mult).then_inc(c.pj.rp, 1)
                    dve.wait_ge(c.pj.rp, rp + 2)
                    dve.tensor_tensor(x32, q_t1, q_t2, ALU.add).then_inc(c.pj.rp, 1)
                    dve.wait_ge(c.pj.rp, rp + 3)
                    stores_wait(dve, c, o)
                    dve.tensor_copy(q_part(o, 0), x32).then_inc(c.pj.rp, 1)
                    rp += 4
                    dve.wait_ge(c.pj.rp, rp)
                    if o.q >= 4:
                        dve.wait_ge(c.pj.low, o.q - 3)
                    dve.tensor_tensor(q_res[o.q % 4], x32, q_part(o, 0), ALU.subtract).then_inc(c.pj.dve, 1)
                    pending.append(o)
                elif o.kind == "V":
                    dst = v_self[:, o.ch * 512:(o.ch + 1) * 512]
                    if c.vbias:
                        dve.tensor_tensor(dst.rearrange("p (t c) -> p t c", t=4), bk.rearrange("p (t c) -> p t c", t=4),
                                          rowv[:, 1, :].unsqueeze(1).to_broadcast([P, 4, C]), ALU.add).then_inc(c.pj.dve, 1)
                    else:
                        dve.tensor_copy(dst, bk).then_inc(c.pj.dve, 1)
                else:
                    dve.tensor_copy(gate[:, 4 * o.ch:4 * o.ch + 4, :],
                                    bk[:, 0:4 * E].rearrange("p (t e) -> p t e", e=E)).then_inc(c.pj.dve, 1)
                if len(pending) > 1:
                    low(pending.pop(0))
            for o in pending:
                low(o)

        def proj_sp(sp, c):
            n = 0
            for o in c.items:
                if o.kind in "QR" and o.q % 2:
                    sp.wait_ge(c.pj.low, o.q + 1)
                    dst, terms = c.stores[o.p]
                    buf = o.q // 2 % 3
                    for t in range(6):
                        sp.dma_start(dst[:, D * t:D * (t + 1), (o.ch - 1) * 512:(o.ch + 1) * 512],
                                     q_parts[buf][:, terms[t], :]).then_inc(c.pj.stored[buf], 16)
                    n = o.q // 2 + 1
            for i in range(3):
                if n > i:
                    sp.wait_ge(c.pj.stored[i], 96 * ((n - i + 2) // 3))

        def stores_wait(eng, c, o):
            if o.q >= 6 and o.q % 2 == 0:
                eng.wait_ge(c.pj.stored[o.q // 2 % 3], 96 * (o.q // 6))

        def q_part(o, a):
            return q_parts[o.q // 2 % 3][:, a, o.q % 2 * 512:(o.q % 2 + 1) * 512]

        def ctx_sems(n):
            class r:
                filled, high, vout = sem(n + "_filled"), sem(n + "_high"), sem(n + "_v")
                res, mid, low, one = sem(n + "_res"), sem(n + "_mid"), sem(n + "_low"), sem(n + "_one")
                loaded = sem(n + "_loaded0"), sem(n + "_loaded1")
                stored = sem(n + "_stored0"), sem(n + "_stored1")

            return r

        def pairs(eng, body):
            for r in range(2):
                body(0, r, True)
            with eng.Fori(1, B // 2) as i:
                for r in range(2):
                    body(i, r, False)

        def nth(c, i, per, k):
            return lin(i + 8 * c.turn, per, k) if c.turn else lin(i, per, k)

        def ctx_pe(pe, c):
            s = c.cx
            pe.wait_ge(s.one, 4 * (1 + c.turn))

            def body(i, r, first):
                pe.wait_ge(s.loaded[r], nth(c, i, 16, 16))
                for k, (k0, n) in enumerate(KCH):
                    if not (first and r == 0):
                        pe.wait_ge(s.res, nth(c, i, 8, 4 * r + k - 3))
                    pe.matmul(psum[:, k, 0:n], wkv[:, 0, :], cx[r][:, k0:k0 + n], start=True, stop=True).then_inc(s.filled, 1)
                for g in range(4):
                    if not (first and r == 0):
                        pe.wait_ge(s.vout, nth(c, i, 8, 4 * r + g - 3))
                    for t in range(4 * g, min(4 * g + 4, KT)):
                        m = P if t < KT - 1 else KLAST
                        last = pe.matmul(psum[0:m, 4 + g, (t % 4) * C:(t % 4 + 1) * C], cx[r][:, t * P:t * P + m],
                                         wkv[:, 1, :], start=True, stop=True)
                    last.then_inc(s.filled, 1)

            pairs(pe, body)

        def ctx_act(act, c):
            s = c.cx

            def middle(i, r, k):
                k0, n = KCH[k]
                act.wait_ge(s.res, nth(c, i, 8, 4 * r + k + 1))
                act.activation(k_parts[r][:, 1, k0:k0 + n], k_res[k][:, 0:n], ACT.Copy).then_inc(s.mid, 1)

            def body(i, r, first):
                if not first:
                    act.wait_ge(s.stored[r], nth(c, i, 80, 0))
                for k, (k0, n) in enumerate(KCH):
                    act.wait_ge(s.filled, nth(c, i, 16, 8 * r + k + 1))
                    act.activation(k_parts[r][:, 0, k0:k0 + n], psum[:, k, 0:n], ACT.Copy).then_inc(s.high, 1)
                    if k:
                        middle(i, r, k - 1)
                middle(i, r, 3)
                for g in range(4):
                    act.wait_ge(s.filled, nth(c, i, 16, 8 * r + 4 + g + 1))
                    m, n = (P, 4) if g < 3 else (KLAST, 1)
                    act.activation(v_st[r][0:m, 4 * g:4 * g + n, :],
                                   psum[0:m, 4 + g, 0:n * C].rearrange("p (t c) -> p t c", c=C), ACT.Copy).then_inc(s.vout, 1)

            pairs(act, body)

        def ctx_dve(dve, c):
            s = c.cx
            for n, (rows, value) in enumerate(((slice(CC, P), 0.0), (slice(CC, CC + 1), 1.0))):
                for r in range(2):
                    dve.memset(cx[r][rows, :], value).then_inc(s.one, 1)
                dve.wait_ge(s.one, 4 * c.turn + 2 * n + 2)

            def low(i, r, k):
                k0, n = KCH[k]
                dve.wait_ge(s.mid, nth(c, i, 8, 4 * r + k + 1))
                dve.tensor_tensor(k_parts[r][:, 2, k0:k0 + n], k_res[k][:, 0:n], k_parts[r][:, 1, k0:k0 + n],
                                  ALU.subtract).then_inc(s.low, 1)

            def body(i, r, first):
                for k, (k0, n) in enumerate(KCH):
                    dve.wait_ge(s.high, nth(c, i, 8, 4 * r + k + 1))
                    if not (first and r == 0):
                        dve.wait_ge(s.low, nth(c, i, 8, 4 * r + k - 3))
                    dve.tensor_tensor(k_res[k][:, 0:n], psum[:, k, 0:n], k_parts[r][:, 0, k0:k0 + n],
                                      ALU.subtract).then_inc(s.res, 1)
                    if k:
                        low(i, r, k - 1)
                low(i, r, 3)

            pairs(dve, body)

        def ctx_sp(sp, c):
            s = c.cx

            def load(i, r):
                if isinstance(i, int):
                    src = A["ctxT"][2 * i + r]
                else:
                    src = A["ctxT"][i * 2 + r]
                sp.dma_start(cx[r][0:CC, :], src).then_inc(s.loaded[r], 16)

            def store(i, r):
                b = i * 2 + r
                sp.wait_ge(s.low, nth(c, i, 8, 4 * r + 4))
                for p in range(3):
                    sp.dma_start(kx_d[b, :, p], k_parts[r][:, p, :]).then_inc(s.stored[r], 16)
                sp.wait_ge(s.vout, nth(c, i, 8, 4 * r + 4))
                full = (KT - 1) * P
                sp.dma_start(vx_d[b, 0:full].rearrange("(t p) c -> p t c", p=P), v_st[r][:, 0:KT - 1, :]).then_inc(s.stored[r], 16)
                sp.dma_start(vx_d[b, full:TC], v_st[r][0:KLAST, KT - 1, :]).then_inc(s.stored[r], 16)

            load(0, 0)
            load(0, 1)

            def body(i, last):
                for r in range(2):
                    if not last:
                        sp.wait_ge(s.filled, nth(c, i, 16, 8 * r + 8))
                        load(i + 1, r)
                    store(i, r)

            with sp.Fori(0, B // 2 - 1) as i:
                body(i, False)
            body(B // 2 - 1, True)
            for r in range(2):
                sp.wait_ge(s.stored[r], 80 * (B // 2) * (1 + c.turn))

        def attn_cfg(c, n):
            c.ns = c.cross + c.self_
            c.NG = KT * c.cross + 2 * c.self_
            c.NT = 2 * c.NG
            c.NS = 16 * c.cross + 4 * c.self_
            c.nm = 2 * c.ns
            c.nv = 2 * c.cross + c.self_

            class s:
                t_filled, p_ready, pv_done = sem(n + "_t_filled"), sem(n + "_p_ready"), sem(n + "_pv_done")
                s_filled, s_free, m_chain = sem(n + "_s_filled"), sem(n + "_s_free"), sem(n + "_m_chain")
                misc_filled, misc_done = sem(n + "_misc_filled"), sem(n + "_misc_done")
                o_evac, o_chain = sem(n + "_o_evac"), sem(n + "_o_chain")
                v_copied, v_loaded = sem(n + "_v_copied"), sem(n + "_v_loaded")

            s.kq_loaded = [sem(f"{n}_kq{g}") for g in range(QUADS)]
            s.m_loaded = [sem(f"{n}_ml{g}") for g in range(QUADS)] if c.cross else []
            c.at = s
            c.nkq = (6 + 2) * c.cross + 4 * c.self_
            c.M_OPS = c.cross + 2 * c.self_ + 4
            c.O_OPS = 2 if c.ns == 1 else 4

        def timeline(c, b, g):
            first, last = (isinstance(b, int) and b == 0), (isinstance(b, int) and b == B - 1)
            NT, NS = c.NT, c.NS
            when = [[] for _ in range(NT)]
            if c.cross:
                for k in range(c.M_OPS):
                    when[1 + k].append(("Ma", k))
                o_at = c.M_OPS + 6
                when[c.M_OPS + 3].append(("Mb",))
                when[o_at].append(("O",))
                for k in range(c.O_OPS + 1):
                    when[o_at + 2 + k].append(("N", k))
                when[o_at + c.O_OPS + 4].append(("Y",))
                when[o_at + c.O_OPS + 7].append(("PR",))
            else:
                when[1].append(("Mb",))
                when[2] += [("O",)] + [("N", k) for k in range(c.O_OPS + 1)]
                when[3] += [("Y",), ("PR",)]
            ev, k = [], 0
            for i in range(NT):
                ev.append(("T", i // 2, i % 2))
                if not c.cross and i == 0 and not (last and g == 3):
                    ev += [("Ma", m) for m in range(c.M_OPS)]
                while k < (i + 1) * NS // NT:
                    if not (last and g >= 2):
                        ev.append(("S", k))
                    k += 1
                if i == 1 and not (first and g == 0):
                    ev += [("PVL",), ("OE",)]
                if i % 2 == 1 and i > 2:
                    ev.append(("PV", i // 2 - 1))
                for name in when[i]:
                    if name[0] in ("Ma", "Mb") and last and g == 3:
                        continue
                    if name[0] in "ON" and first and g == 0:
                        continue
                    if name[0] in ("Y", "PR") and (g != 0 or first):
                        continue
                    ev.append(name)
            return ev

        TAIL = [("PVL",), ("OE",), ("O",), ("Y",), ("PR",)]

        def misc_index(b, g, kind):
            if isinstance(b, int) and b == 0:
                return {"Mb": [1, 2, 4, 6][g], "O": [None, 3, 5, 7][g]}[kind]
            if g == 4:
                return lin(b, 10, -2 + 9 + ["O", "Y", "PR"].index(kind))
            if g == 0:
                return lin(b, 10, -2 + ["Mb", "O", "Y", "PR"].index(kind))
            off = 4 + 2 * (g - 1)
            if isinstance(b, int) and b == B - 1 and g == 3:
                return lin(b, 10, -2 + off)
            return lin(b, 10, -2 + off + (kind == "O"))

        def ahead(b, g, k):
            g2 = g + k
            return (b + g2 // 4 if g2 // 4 else b), g2 % 4

        def steps(eng, emit):
            for g in range(QUADS):
                emit(0, g)
            with eng.Fori(1, B - 1) as b:
                for g in range(QUADS):
                    emit(b, g)
            for g in range(QUADS):
                emit(B - 1, g)

        def misc_bank():
            return psum[:, 7, :]

        def seg(c, u):
            if u >= KT * c.cross:
                own = u - KT * c.cross
                return own, None, P, T - P * own
            return None, u, (P if u < KT - 1 else KLAST), T

        def attn_pe(pe, c):
            s = c.at

            def s_unit(b, g, k):
                idx_c = g * c.NS + k
                if k == 0:
                    pe.wait_ge(s.kq_loaded[g], lin(b, 16 * c.nkq, 16 * c.nkq))
                if not (isinstance(b, int) and b == 0 and idx_c < 2):
                    pe.wait_ge(s.s_free, lin(b, QUADS * c.NS, idx_c - 1))
                bk = 2 * (idx_c % 2)
                if c.cross and k < 16:
                    j, qt, half = k // 4, k // 2 % 2, k % 2
                    e, hp = j % 2, j // 2
                    for m in range(2):
                        k0 = SSTART[2 * half + m]
                        last = pe.matmul(psum[:, bk + m, 0:SC], qst[:, g, hp, e, qt * P:(qt + 1) * P],
                                         kst[:, g, hp, k0:k0 + SC], start=True, stop=True)
                else:
                    j = k - 16 * c.cross
                    e, hp = j % 2, j // 2
                    ps = psum[:, bk, :]
                    pe.matmul(ps[:, 0:P], qss[:, g, hp, e, 0:P], kss[:, g, hp, 0:P], start=True, stop=False,
                              skip_group_check=True)
                    pe.matmul(ps[:, 0:P], ident16[:, :], mask_qk[:, :], start=False, stop=True, skip_group_check=True)
                    pe.matmul(ps[:, P:3 * P], qss[:, g, hp, e, P:T], kss[:, g, hp, :], start=True, stop=False,
                              skip_group_check=True)
                    last = pe.matmul(ps[:, 2 * P:3 * P], ident16[:, :], mask_qk[:, :], start=False, stop=True,
                                     skip_group_check=True)
                last.then_inc(s.s_filled, 1)

            def t_unit(b, g, u, hp):
                idx_c = g * c.NT + 2 * u + hp
                if u == 0 and hp == 0:
                    if c.cross:
                        pe.wait_ge(s.m_loaded[g], lin(b, 16 * c.nm, 16 * c.nm))
                    elif isinstance(b, int) and b == 0 and g == 0:
                        pe.wait_ge(s.misc_done, 1)
                    else:
                        pe.wait_ge(s.misc_done, misc_index(*((b, g - 1) if g else (b - 1, 3)), "Mb") + 1)
                if not (isinstance(b, int) and b == 0 and idx_c < 2):
                    pe.wait_ge(s.p_ready, lin(b, QUADS * c.NT, idx_c - 1))
                own, t, m, n = seg(c, u)
                ps = psum[0:m, 4 + idx_c % 2, 0:2 * n].rearrange("p (e q) -> p e q", e=2)
                if own is not None:
                    pe.matmul(ps, kss[:, g, hp, own * P:(own + 1) * P], qss[:, g, hp, :, own * P:T], start=True, stop=False,
                              skip_group_check=True)
                    last = pe.matmul(ps[:, :, 0:P], ident16[:, :], mask_kq[:, :].unsqueeze(1).to_broadcast([P, 2, P]),
                                     start=False, stop=bool(c.cross), skip_group_check=True)
                    if not c.cross:
                        for e in range(2):
                            last = pe.matmul(ps[:, e, :], pick[:, hp, e, :], mrow[:, g % 2, own * P:T], start=False,
                                             stop=(e == 1), skip_group_check=True)
                else:
                    last = pe.matmul(ps, kst[:, g, hp, t * P:t * P + m], qst[:, g, hp, :, :], start=True, stop=True)
                last.then_inc(s.t_filled, 1)

            def pv_unit(b, g, u):
                pe.wait_ge(s.p_ready, lin(b, QUADS * c.NT, g * c.NT + 2 * u + 2))
                if u == 0:
                    pe.wait_ge(s.v_copied, lin(b, QUADS * c.nv, c.nv * (g + 1)))
                    if not (isinstance(b, int) and b == 0 and g == 0):
                        pe.wait_ge(s.o_evac, lin(b, QUADS, g))
                pr = p_ring[:, (g * c.NG + u) % 4]
                own, t, m, n = seg(c, u)
                for j in range(4):
                    if own is not None:
                        o0 = T * c.cross + own * P
                        last = pe.matmul(psum[32 * j:32 * j + VC, 6, o0:o0 + n], vs[:, g % 2, own, j, :], pr[:, j, 0:n],
                                         start=(own == 0), stop=(own == 1), skip_group_check=True)
                    else:
                        last = pe.matmul(psum[32 * j:32 * j + VC, 6, 0:T], vq[0:m, g % 2, t, j, :], pr[0:m, j, :],
                                         start=(t == 0), stop=(t == KT - 1), skip_group_check=True)
                last.then_inc(s.pv_done, 1)

            def emit(b, g, events=None):
                for ev in events or timeline(c, b, g):
                    kind = ev[0]
                    if kind == "T":
                        t_unit(b, g, ev[1], ev[2])
                    elif kind == "S":
                        b2, g2 = ahead(b, g, 2)
                        s_unit(b2, g2, ev[1])
                    elif kind == "PV":
                        pv_unit(b, g, ev[1])
                    elif kind == "PVL":
                        b2, g2 = (b, g - 1) if g else (b - 1, 3)
                        pv_unit(b2, g2, c.NG - 1)
                    elif kind == "Mb":
                        m_turn(b, g, misc_index(b, g, "Mb"), *ahead(b, g, 1))
                    elif kind == "O":
                        i = misc_index(b, g, "O")
                        pe.wait_ge(s.misc_done, i)
                        pe.wait_ge(s.o_evac, lin(b, QUADS, g))
                        for k in range(2 * c.ns):
                            last = pe.transpose(misc_bank()[:, k * P:(k + 1) * P], osb[:, k * P:(k + 1) * P], ident[:, :])
                        last.then_inc(s.misc_filled, 1)
                    elif kind == "Y":
                        i = misc_index(b, g, "Y")
                        pe.wait_ge(s.misc_done, i)
                        pe.wait_ge(s.o_chain, lin(b, QUADS * c.O_OPS, g // 4 * QUADS * c.O_OPS))
                        for k in range(2):
                            last = pe.transpose(misc_bank()[:, k * P:(k + 1) * P], yb[:, k, :], ident[:, :])
                        last.then_inc(s.misc_filled, 1)
                    elif kind == "PR":
                        i = misc_index(b, g, "PR")
                        pe.wait_ge(s.misc_done, i)
                        for k in range(2):
                            last = pe.matmul(misc_bank()[:, k * C:(k + 1) * C], yT[:, k * P:(k + 1) * P], c.wo,
                                             start=True, stop=True)
                        last.then_inc(s.misc_filled, 1)

            def m_turn(b, g, i, bm, gm):
                if not (isinstance(i, int) and i == 0):
                    pe.wait_ge(s.misc_done, i)
                pe.wait_ge(s.m_chain, lin(bm, QUADS * c.M_OPS, c.M_OPS * (gm + 1)))
                mb = misc_bank().bitcast(BF16)
                n = 12 * c.ns
                for qt in range(2):
                    last = pe.transpose(mb[0:n, qt * P:(qt + 1) * P], mpt[:, qt * n:(qt + 1) * n], ident16[:, :])
                last.then_inc(s.misc_filled, 1)

            for k in range(c.NS):
                s_unit(0, 0, k)
            m_turn(0, 0, 0, 0, 0)
            for k in range(c.NS):
                s_unit(0, 1, k)
            steps(pe, emit)
            emit(B, 0, TAIL[:1])
            emit(B - 1, 4, TAIL[1:])

        def attn_act(act, c):
            s = c.at

            def emit(b, g, events=None):
                for ev in events or timeline(c, b, g):
                    if ev[0] == "T":
                        u, hp = ev[1], ev[2]
                        idx_c = g * c.NT + 2 * u + hp
                        grp = g * c.NG + u
                        act.wait_ge(s.t_filled, lin(b, QUADS * c.NT, idx_c + 1))
                        if hp == 0 and not (isinstance(b, int) and b == 0 and grp < 4):
                            act.wait_ge(s.pv_done, lin(b, QUADS * c.NG, grp - 3))
                        _, _, m, n = seg(c, u)
                        act.activation(p_ring[0:m, grp % 4, 2 * hp:2 * hp + 2, 0:n],
                                       psum[0:m, 4 + idx_c % 2, 0:2 * n].rearrange("p (e q) -> p e q", e=2), ACT.Exp,
                                       scale=SCALE).then_inc(s.p_ready, 1)
                    elif ev[0] == "OE":
                        act.wait_ge(s.pv_done, lin(b, QUADS * c.NG, g * c.NG))
                        if not (isinstance(b, int) and b == 0 and g <= 1):
                            bp, gp = (b, g - 1) if g else (b - 1, 3)
                            act.wait_ge(s.misc_filled, prev_o(bp, gp) + 1)
                        n = T * c.ns
                        act.activation(osb[:, 0:n], psum[:, 6, 0:n], ACT.Copy).then_inc(s.o_evac, 1)

            def prev_o(bp, gp):
                return misc_index(bp, gp, "O") if not (isinstance(bp, int) and bp == 0 and gp == 0) else 0

            steps(act, emit)
            act.wait_ge(s.pv_done, B * QUADS * c.NG)
            act.wait_ge(s.misc_filled, misc_index(B - 1, 3, "O") + 1)
            act.activation(osb[:, 0:T * c.ns], psum[:, 6, 0:T * c.ns], ACT.Copy).then_inc(s.o_evac, 1)

        def attn_dve(dve, c):
            s = c.at

            def s_max(b, g, k):
                idx_c = g * c.NS + k
                dve.wait_ge(s.s_filled, lin(b, QUADS * c.NS, idx_c + 1))
                bk = 2 * (idx_c % 2)
                if c.cross and k < 16:
                    j, qt, half = k // 4, k // 2 % 2, k % 2
                    je = (j % 2) * 2 + j // 2
                    dve.tensor_reduce(mp[:, g % 2, half, qt, je:je + 1], psum[:, bk:bk + 2, 0:SC], AX.XY, ALU.max)\
                       .then_inc(s.s_free, 1)
                else:
                    j = k - 16 * c.cross
                    je = (j % 2) * 2 + j // 2
                    dve.tensor_reduce(mps[:, g % 2, :, je], psum[:, bk, 0:3 * P].rearrange("p (a n) -> p a n", a=3),
                                      AX.X, ALU.max).then_inc(s.s_free, 1)

            def m_part(b, g, k):
                if k == 0:
                    dve.wait_ge(s.s_free, lin(b, QUADS * c.NS, (g + 1) * c.NS))
                else:
                    dve.wait_ge(s.m_chain, lin(b, QUADS * c.M_OPS, g * c.M_OPS + k))
                par, so = g % 2, c.ns - 1
                pt = mpt[:, 0:24 * c.ns].rearrange("p (q s e a h) -> p q s e a h", q=2, s=c.ns, e=2, a=3)

                def part(a):
                    return pt[:, :, :, :, a, :].rearrange("p q s e h -> p (q s e) h")

                what = (["halves"] * c.cross + ["first", "second"] * c.self_ + ["high", "rest", "middle", "low"])[k]
                if what == "halves":
                    ins = dve.tensor_tensor(mx[:, :, 0, :], mp[:, par, 0], mp[:, par, 1], ALU.max)
                elif what == "first":
                    ins = dve.tensor_copy(mx[:, 0, so, :], mps[:, par, 0, :])
                elif what == "second":
                    ins = dve.tensor_tensor(mx[:, 1, so, :], mps[:, par, 1, :], mps[:, par, 2, :], ALU.max)
                elif what == "high":
                    ins = dve.tensor_scalar(part(0), flat2(c, mx), -1.0, None, ALU.mult)
                elif what == "rest":
                    ins = dve.scalar_tensor_tensor(flat2(c, mr), flat2(c, mx), -1.0, part(0), ALU.mult, ALU.subtract)
                elif what == "middle":
                    ins = dve.tensor_copy(part(1), flat2(c, mr))
                else:
                    ins = dve.tensor_tensor(part(2), flat2(c, mr), part(1), ALU.subtract)
                ins.then_inc(s.m_chain, 1)

            def flat2(c, tile):
                if c.ns == 2:
                    return tile[:, :, :, :].rearrange("p q s (e h) -> p (q s e) h", e=2)
                return tile[:, :, 0, :].rearrange("p q (e h) -> p q e h", e=2)

            def m_rows(i, b, g):
                dve.wait_ge(s.misc_filled, i + 1)
                if not (isinstance(b, int) and b == 0 and g < 2):
                    b2, g2 = (b, g - 2) if g >= 2 else (b - 1, g + 2)
                    if c.cross:
                        dve.wait_ge(s.m_loaded[g2], lin(b2, 16 * c.nm, 16 * c.nm))
                    else:
                        dve.wait_ge(s.t_filled, lin(b2, QUADS * c.NT, (g2 + 1) * c.NT))
                n = 12 * c.ns
                dve.tensor_copy(mrow[0:n, g % 2, :], misc_bank().bitcast(BF16)[0:n, 0:T]).then_inc(s.misc_done, 1)

            def o_norm(i, b, g, gq, k):
                base = lin(b, QUADS * c.O_OPS, (g - 1) * c.O_OPS)
                bank = misc_bank()
                if k == 0:
                    dve.wait_ge(s.misc_filled, i + 1)
                    den = bank[:, 0:256 * c.ns].rearrange("p (n c) -> p n c", c=VC)[:, :, D]
                    dve.reciprocal(rec[:, 0:8 * c.ns], den).then_inc(s.o_chain, 1)
                elif k <= c.ns:
                    dve.wait_ge(s.o_chain, base + 1)
                    a = k - 1
                    num = bank[:, 256 * a:256 * (a + 1)].rearrange("p (q j c) -> p q j c", q=2, j=4)[:, :, :, 0:D]
                    r = rec[:, 8 * a:8 * a + 8].rearrange("p (q j) -> p q j", q=2).unsqueeze(3).to_broadcast([P, 2, 4, D])
                    dst = (yb, yb2)[a][:, :, 32 * gq:32 * gq + 32].rearrange("p q (j d) -> p q j d", j=4)
                    dve.tensor_tensor(dst, num, r, ALU.mult).then_inc(s.o_chain, 1)
                elif k < c.O_OPS:
                    dve.wait_ge(s.o_chain, base + 3)
                    ys = yb[:, :, 32 * gq:32 * gq + 32]
                    dve.tensor_tensor(ys, ys, yb2[:, :, 32 * gq:32 * gq + 32], ALU.add).then_inc(s.o_chain, 1)
                else:
                    dve.wait_ge(s.o_chain, base + c.O_OPS)
                    dve.sem_inc(s.misc_done, 1)

            def emit(b, g, events=None):
                for ev in events or timeline(c, b, g):
                    kind = ev[0]
                    if kind == "S":
                        s_max(*ahead(b, g, 2), ev[1])
                    elif kind == "Ma":
                        m_part(*ahead(b, g, 1), ev[1])
                    elif kind == "Mb":
                        m_rows(misc_index(b, g, "Mb"), *ahead(b, g, 1))
                    elif kind == "N":
                        o_norm(misc_index(b, g, "O"), b, g, (g - 1) % 4, ev[1])
                    elif kind == "Y":
                        dve.wait_ge(s.misc_filled, misc_index(b, g, "Y") + 1)
                        dve.tensor_copy(yT[:, :], misc_bank()[:, 0:T]).then_inc(s.misc_done, 1)
                    elif kind == "PR":
                        dve.wait_ge(s.misc_filled, misc_index(b, g, "PR") + 1)
                        xs = x[:, bass.ds((b - 1) * T, T)] if not isinstance(b, int) else x[:, (b - 1) * T:b * T]
                        dve.tensor_tensor(xs, misc_bank()[:, 0:T], xs, ALU.add).then_inc(s.misc_done, 1)

            for k in range(c.NS):
                s_max(0, 0, k)
            for k in range(c.M_OPS):
                m_part(0, 0, k)
            m_rows(0, 0, 0)
            for k in range(c.NS):
                s_max(0, 1, k)
            steps(dve, emit)
            for k in range(c.O_OPS + 1):
                o_norm(misc_index(B - 1, 4, "O"), B - 1, 4, 3, k)
            dve.wait_ge(s.misc_filled, misc_index(B - 1, 4, "Y") + 1)
            dve.tensor_copy(yT[:, :], misc_bank()[:, 0:T]).then_inc(s.misc_done, 1)
            dve.wait_ge(s.misc_filled, misc_index(B - 1, 4, "PR") + 1)
            xs = x[:, (B - 1) * T:B * T]
            dve.tensor_tensor(xs, misc_bank()[:, 0:T], xs, ALU.add).then_inc(s.misc_done, 1)

        def attn_pads(pool, c):
            def put(ins):
                count["made"] += 1
                ins.then_inc(made, 1)
                pool.wait_ge(made, count["made"])

            for tile in ([qst] if c.cross else []) + ([qss] if c.self_ else []):
                put(pool.memset(tile[:, :, :, :, :], 0.0))
            if c.name == "a":
                for tile in (kst, kss):
                    for e in range(2):
                        put(pool.memset(tile[64 * e + 32:64 * e + 64, :, :, :], 1.0))

        def attn_pool(pool, c):
            s = c.at
            for tile in ([vq] if c.cross else []) + ([vs] if c.self_ else []):
                pool.memset(tile[:, :, :, :, :], 0.0).then_inc(made, 1)
                pool.wait_ge(made, count["made"] + 1)
                for r in range(2):
                    pool.memset(tile[:, r, :, :, D:D + 1], 1.0).then_inc(made, 1)
                count["made"] += 3
                pool.wait_ge(made, count["made"])

            def copies(b, g):
                r = g % 2
                if c.cross:
                    if g == 0:
                        pool_wait(pool, s.v_loaded, lin(b, 32, 32))
                    v = vb[:, :, 32 * g:32 * g + 32].rearrange("p t (j d) -> p t j d", j=4)
                    pool.tensor_copy(vq[:, r, 0:KT - 1, :, 0:D], v[:, 0:KT - 1]).then_inc(s.v_copied, 1)
                    pool.tensor_copy(vq[0:KLAST, r, KT - 1, :, 0:D], v[0:KLAST, KT - 1]).then_inc(s.v_copied, 1)
                if c.self_:
                    src = v_self[:, b * T:(b + 1) * T] if isinstance(b, int) else v_self[:, bass.ds(b * T, T)]
                    v = src.rearrange("p (k c) -> p k c", k=2)[:, :, 32 * g:32 * g + 32]\
                        .rearrange("p k (j d) -> p k j d", j=4)
                    pool.tensor_copy(vs[:, r, :, :, 0:D], v).then_inc(s.v_copied, 1)

            copies(0, 0)

            def emit(b, g):
                if isinstance(b, int) and b == B - 1 and g == 3:
                    return
                if not (isinstance(b, int) and b == 0 and g == 0):
                    pool_wait(pool, s.pv_done, lin(b, QUADS * c.NG, g * c.NG))
                copies(*ahead(b, g, 1))

            steps(pool, emit)

        def attn_sp(sp, c):
            s = c.at

            def col(b):
                return slice(b * T, (b + 1) * T) if isinstance(b, int) else bass.ds(b * T, T)

            def heads(g, e):
                return slice(4 * g + e, 4 * g + 4, 2)

            def quad_loads(b, g):
                q = s.kq_loaded[g]
                for e in range(2):
                    r0 = 64 * e
                    if c.cross:
                        kx = kx_d[b]
                        for t, n in ((0, 3), (3, 2), (5, 1)):
                            sp.dma_start(kst[r0 + D * t:r0 + D * (t + n), g, :, :],
                                         kx[heads(g, e), 0:n].rearrange("h p d n -> (p d) h n")).then_inc(q, 16)
                        sp.dma_start(qst[r0:r0 + ROWSM, g, :, e, :],
                                     qx_d[heads(g, e), :, col(b)].rearrange("h r n -> r h n")).then_inc(q, 16)
                    if c.self_:
                        sp.dma_start(qss[r0:r0 + ROWSM, g, :, e, :],
                                     qs_d[heads(g, e), :, col(b)].rearrange("h r n -> r h n")).then_inc(q, 16)
                        sp.dma_start(kss[r0:r0 + ROWS, g, :, :],
                                     ks_d[heads(g, e), :, col(b)].rearrange("h r n -> r h n")).then_inc(q, 16)

            def m_load(i, b, g):
                sp.wait_ge(s.misc_done, i + 1)
                for k in range(c.ns):
                    dst = (qst if c.cross and k == 0 else qss)
                    for e in range(2):
                        sp.dma_start(dst[64 * e + ROWS:64 * e + ROWSM, g, :, e, :],
                                     mrow[12 * k + 6 * e:12 * k + 6 * e + 6, g % 2, :]).then_inc(s.m_loaded[g], 16)

            def v_load(b):
                v = vx_d[b]
                full = (KT - 1) * P
                sp.dma_start(vb[:, 0:KT - 1, :], v[0:full].rearrange("(t p) c -> p t c", p=P)).then_inc(s.v_loaded, 16)
                sp.dma_start(vb[0:KLAST, KT - 1, :], v[full:TC]).then_inc(s.v_loaded, 16)

            quad_loads(0, 0)
            quad_loads(0, 1)
            if c.cross:
                v_load(0)
            quad_loads(0, 2)
            if c.cross:
                m_load(0, 0, 0)
            quad_loads(0, 3)

            def emit(b, g):
                last = isinstance(b, int) and b == B - 1
                if c.cross and not (last and g == 3):
                    m_load(misc_index(b, g, "Mb"), *ahead(b, g, 1))
                if last:
                    return
                sp.wait_ge(s.t_filled, lin(b, QUADS * c.NT, (g + 1) * c.NT))
                quad_loads(b + 1, g)
                if g == 2 and c.cross:
                    sp.wait_ge(s.v_copied, lin(b, QUADS * c.nv, QUADS * c.nv))
                    v_load(b + 1)

            steps(sp, emit)

        g_a = arenaB[:, 0:256].rearrange("p (t e) -> p t e", e=E)
        g_b = arenaB[:, 256:512].rearrange("p (t e) -> p t e", e=E)
        g_1 = arenaB[:, 512:768].rearrange("p (t e) -> p t e", e=E)
        g_2 = arenaB[:, 768:1024].rearrange("p (t e) -> p t e", e=E)
        g_c = arenaB[:, 1024:1280].rearrange("p (t e) -> p t e", e=E)
        g_s = arenaB[:, 1280:1312]
        g_m = arenaB[:, 1536:1792].rearrange("p (t e) -> p t e", e=E)
        gT = arenaB[0:E, 4096:8192]

        def bc(a):
            return a.unsqueeze(2).to_broadcast([P, TILES, E])

        def gate_sems(n):
            class r:
                dve, act, pe = sem(n + "_gt_dve"), sem(n + "_gt_act"), sem(n + "_gt_pe")
                b2, turned = sem(n + "_gt_b2"), sem(n + "_gt_turned")

            return r

        def gates_dve(dve, c):
            s = c.gt
            k = [0]

            def link(ins):
                k[0] += 1
                ins.then_inc(s.dve, 1)
                dve.wait_ge(s.dve, k[0])

            tt, L = dve.tensor_tensor, gate[:, :, :]
            link(dve.tensor_reduce(g_s, L, AX.X, ALU.max))
            link(tt(g_a, L, bc(g_s), ALU.subtract))
            dve.wait_ge(s.act, 1)
            link(dve.tensor_reduce(g_s, g_b, AX.X, ALU.add))
            link(dve.reciprocal(g_s, g_s))
            link(tt(L, g_b, bc(g_s), ALU.mult))
            for one, src in ((g_1, L), (g_2, g_a)):
                link(dve.tensor_reduce(g_s, src, AX.X, ALU.max))
                link(tt(g_b, src, bc(g_s), ALU.is_equal))
                link(tt(g_b, g_b, rank[:, :, :], ALU.mult))
                link(dve.tensor_reduce(g_s, g_b, AX.X, ALU.max))
                link(tt(one, g_b, bc(g_s), ALU.is_equal))
                if one is g_1:
                    link(dve.scalar_tensor_tensor(g_a, g_1, -2.0, L, ALU.mult, ALU.add))
            link(tt(g_m, g_1, g_2, ALU.add))
            link(tt(L, L, g_m, ALU.mult))
            c.mask_made = k[0]
            if c.capacity:
                dve.wait_ge(s.pe, 2)
                tot = psum[:, 1, 0:256].rearrange("p (t e) -> p t e", e=E)
                link(dve.memset(g_a, 0.0))
                link(dve.tensor_copy(g_a[:, 1:TILES, :], tot[:, 0:TILES - 1, :]))
                src, dst = g_a, g_b
                step = 1
                while step < TILES:
                    link(dve.tensor_copy(dst[:, 0:step, :], src[:, 0:step, :]))
                    link(tt(dst[:, step:, :], src[:, step:, :], src[:, 0:TILES - step, :], ALU.add))
                    src, dst = dst, src
                    step *= 2
                link(tt(g_c, psum[:, 0, 0:256].rearrange("p (t e) -> p t e", e=E), src, ALU.add))
                link(dve.tensor_scalar(g_c, g_c, float(CAP), None, ALU.is_le))
                link(tt(L, L, g_c, ALU.mult))
            c.gates_made = k[0]
            for ch in range(CHUNKS):
                dve.wait_ge(s.turned, ch + 1)
                dve.tensor_copy(gT[:, ch * 512:(ch + 1) * 512], psum[0:E, ch, :]).then_inc(s.b2, 1)
            for ch in range(CHUNKS):
                dve.wait_ge(s.turned, CHUNKS + ch + 1)
                xs = x[:, ch * 512:(ch + 1) * 512]
                dve.tensor_tensor(xs, psum[:, ch, :], xs, ALU.add).then_inc(s.b2, 1)

        def gates_act(act, c):
            act.wait_ge(c.gt.dve, 2)
            act.activation(g_b, g_a, ACT.Exp).then_inc(c.gt.act, 1)

        MASK_LINKS = 5 + 6 + 5 + 2

        def gates_pe(pe, c):
            s = c.gt
            pe.wait_ge(s.dve, MASK_LINKS)
            m = g_m.rearrange("p t e -> p (t e)")
            total = MASK_LINKS
            if c.capacity:
                pe.matmul(psum[:, 0, 0:256], upper[:, :], m, start=True, stop=True).then_inc(s.pe, 1)
                pe.matmul(psum[:, 1, 0:256], ones[:, :], m, start=True, stop=True).then_inc(s.pe, 1)
                total += 2 + 10 + 3
            pe.wait_ge(s.dve, total)
            for ch in range(CHUNKS):
                for t in range(4):
                    last = pe.transpose(psum[0:E, ch, t * P:(t + 1) * P], gate[:, 4 * ch + t, :], ident[:, :])
                last.then_inc(s.turned, 1)
            for ch in range(CHUNKS):
                pe.wait_ge(s.b2, ch + 1)
                for t in range(4):
                    last = pe.matmul(psum[:, ch, t * C:(t + 1) * C], gT[:, (4 * ch + t) * P:(4 * ch + t + 1) * P], b2s[:, :],
                                     start=True, stop=True)
                last.then_inc(s.turned, 1)

        w_raw = arenaA[:, :].rearrange("p (m e k f) -> p m e k f", m=3, e=E, k=FC)
        w_in = arenaA[:, 0:4096]
        w_up = arenaA[:, 4096:8192]
        w_out = arenaA[:, 8192:12288].rearrange("p (e k c) -> p e k c", e=E, k=FC)
        f_y = [arenaB[:, 512 * i:512 * (i + 1)] for i in range(2)]
        f_h = [arenaB[:, 1024 + 512 * i:1024 + 512 * (i + 1)] for i in range(4)]
        gcol = gch[:, :, :].rearrange("p t e -> p (t e)")
        gtail = stat[:, 0, 0:4]
        bias_in, bias_up = stat[:, 0, 4:4 + FC], stat[:, 0, 8:8 + FC]
        NQ = CHUNKS * FC

        def ffn_sems(n):
            class r:
                g, u, y, h, o = sem(n + "_g"), sem(n + "_u"), sem(n + "_y"), sem(n + "_h"), sem(n + "_o")
                acc, gch = sem(n + "_acc"), sem(n + "_gch")
                bias = sem(n + "_bias")
                xhi, xlo, whi, wlo = sem(n + "_xhi"), sem(n + "_xlo"), sem(n + "_whi"), sem(n + "_wlo")

            return r

        def experts(eng, body):
            body(0, True, False)
            with eng.Fori(1, E - 1) as e:
                body(e, False, False)
            body(E - 1, False, True)

        def one(e):
            return slice(e, e + 1) if isinstance(e, int) else bass.ds(e, 1)

        def raw(c, e, k):
            return w_raw[:, 0:1 + c.gated, one(e), k, :]

        def ffn_pe(pe, c):
            s = c.ff

            def down(e, first, q):
                ch, k = q // FC, q % FC
                pe.wait_ge(s.h, nth(c, e, NQ, q + 1))
                if k == 0 and not (first and ch < 2):
                    pe.wait_ge(s.acc, nth(c, e, CHUNKS, ch - 1))
                for t in range(4):
                    last = pe.matmul(psum[:, 4 + ch % 2, t * C:(t + 1) * C], f_h[q % 4][:, t * P:(t + 1) * P],
                                     w_out[:, one(e), k, :].rearrange("p e c -> p (e c)"), start=(k == 0 and t == 0),
                                     stop=(k == FC - 1), skip_group_check=True)
                last.then_inc(s.o, 1)

            def up(m, bank, ch, k, done):
                r = ch % 2
                pe.matmul(psum[:, bank, :], wh[:, k, m, :], xl[:, r, :], start=True, stop=False)
                pe.matmul(psum[:, bank, :], wl[:, k, m, :], xh[:, r, :], start=False, stop=False)
                pe.matmul(psum[:, bank, :], wh[:, k, m, :], xh[:, r, :], start=False, stop=True).then_inc(done, 1)

            def body(e, first, last):
                for q in range(NQ):
                    ch, k = q // FC, q % FC
                    if k == 0:
                        pe.wait_ge(s.xlo, nth(c, e, CHUNKS, ch + 1))
                    if ch == 0:
                        pe.wait_ge(s.wlo, nth(c, e, FC, k + 1))
                    if not (first and q < 2):
                        pe.wait_ge(s.y if c.gated else s.h, nth(c, e, NQ, q - 1))
                    up(0, q % 2, ch, k, s.g)
                    if c.gated:
                        if not (first and q < 2):
                            pe.wait_ge(s.h, nth(c, e, NQ, q - 1))
                        up(1, 2 + q % 2, ch, k, s.u)
                    if q:
                        down(e, first, q - 1)
                    elif not first:
                        down(e - 1, False, NQ - 1)
                if last:
                    down(e, False, NQ - 1)

            experts(pe, body)

        def ffn_act(act, c):
            s = c.ff

            def x_high(ch):
                act.activation(xh[:, ch % 2, :], xnT[:, ch * 512:(ch + 1) * 512], ACT.Copy).then_inc(s.xhi, 1)

            def w_high(e, k):
                act.activation(wh[:, k, 0:1 + c.gated, :].unsqueeze(2), raw(c, e, k), ACT.Copy).then_inc(s.whi, 1)

            def body(e, first, last):
                if not first:
                    act.wait_ge(s.y if c.gated else s.h, nth(c, e, NQ, 0))
                act.activation(bias_in.unsqueeze(1), b1s[:, 0, one(e), :], ACT.Copy).then_inc(s.bias, 1)
                act.wait_ge(s.bias, nth(c, e, 1, 1))
                for q in range(NQ):
                    ch, k = q // FC, q % FC
                    act.wait_ge(s.g, nth(c, e, NQ, q + 1))
                    if c.gated:
                        if not (first and q < 2):
                            act.wait_ge(s.h, nth(c, e, NQ, q - 1))
                        act.activation(f_y[q % 2], psum[:, q % 2, :], ACT.Gelu, bias=bias_in[:, k:k + 1])\
                           .then_inc(s.y, 1)
                    else:
                        if not (first and q < 4):
                            act.wait_ge(s.o, nth(c, e, NQ, q - 3))
                        act.activation(f_h[q % 4], psum[:, q % 2, :], ACT.Gelu, bias=bias_in[:, k:k + 1])\
                           .then_inc(s.h, 1)
                    if k == 1 and not (last and ch == CHUNKS - 1):
                        if c.gated and not (first and ch == 0):
                            act.wait_ge(s.u, nth(c, e, NQ, FC * ch))
                        x_high((ch + 1) % CHUNKS)
                    if ch == CHUNKS - 1 and not last:
                        if c.gated:
                            act.wait_ge(s.u, nth(c, e, NQ, q + 1))
                        w_high(e + 1, k)

            for k in range(FC):
                w_high(0, k)
            x_high(0)
            experts(act, body)

        def ffn_dve(dve, c):
            s = c.ff

            def taken(e, k):
                return lin(e, 2 + c.gated, k + 3 * E * c.turn)

            def x_low(e, ch):
                dve.wait_ge(s.xhi, nth(c, e, CHUNKS, ch + 1))
                r = ch % 2
                dve.tensor_tensor(xl[:, r, :], xnT[:, ch % CHUNKS * 512:(ch % CHUNKS + 1) * 512], xh[:, r, :], ALU.subtract)\
                   .then_inc(s.xlo, 1)

            def w_low(e, k):
                dve.wait_ge(s.whi, nth(c, e, FC, k + 1))
                high = wh[:, k, 0:1 + c.gated, :].unsqueeze(2)
                dve.tensor_tensor(wl[:, k, 0:1 + c.gated, :].unsqueeze(2), raw(c, e, k), high, ALU.subtract)\
                   .then_inc(s.wlo, 1)

            def add_up(e, first, ch, gates):
                dve.wait_ge(s.o, nth(c, e, NQ, FC * (ch + 1)))
                if not (first and ch == 0):
                    dve.wait_ge(s.acc, nth(c, e, CHUNKS, ch))
                for t in range(4):
                    xs = x[:, ch * 512 + t * P:ch * 512 + (t + 1) * P]
                    last = dve.scalar_tensor_tensor(xs, psum[:, 4 + ch % 2, t * C:(t + 1) * C], gates[:, t:t + 1], xs,
                                                    ALU.mult, ALU.add)
                last.then_inc(s.acc, 1)

            def body(e, first, last):
                if not first:
                    dve.wait_ge(s.acc, nth(c, e, CHUNKS, -1))
                    dve.tensor_copy(gtail, gcol[:, TILES - 4:TILES]).then_inc(s.gch, 1)
                else:
                    dve.tensor_copy(gtail, gate[:, 0:4, 0]).then_inc(s.gch, 1)
                dve.wait_ge(s.gch, taken(e, 1))
                dve.tensor_copy(gcol.unsqueeze(2), gate[:, :, one(e)]).then_inc(s.gch, 1)
                if c.gated:
                    if not first:
                        dve.wait_ge(s.h, nth(c, e, NQ, 0))
                    dve.tensor_copy(bias_up.unsqueeze(1), b1s[:, 1, one(e), :]).then_inc(s.gch, 1)
                dve.wait_ge(s.gch, taken(e, 2 + c.gated))
                for q in range(NQ):
                    ch, k = q // FC, q % FC
                    if c.gated:
                        dve.wait_ge(s.u, nth(c, e, NQ, q + 1))
                        dve.wait_ge(s.y, nth(c, e, NQ, q + 1))
                        if not (first and q < 4):
                            dve.wait_ge(s.o, nth(c, e, NQ, q - 3))
                        dve.scalar_tensor_tensor(f_h[q % 4], psum[:, 2 + q % 2, :], bias_up[:, k:k + 1], f_y[q % 2],
                                                 ALU.add, ALU.mult).then_inc(s.h, 1)
                    if k == 1:
                        if not (last and ch == CHUNKS - 1):
                            x_low(e, ch + 1)
                        if ch:
                            add_up(e, first, ch - 1, gcol[:, 4 * (ch - 1):4 * ch])
                        elif not first:
                            add_up(e - 1, False, CHUNKS - 1, gtail)
                    if ch == CHUNKS - 1 and not last:
                        w_low(e + 1, k)
                if last:
                    add_up(e, False, CHUNKS - 1, gcol[:, TILES - 4:TILES])

            for k in range(FC):
                w_low(0, k)
            x_low(0, 0)
            experts(dve, body)

        def W(i):
            return wbig[:, i, :]

        c1 = Part(cross=1, self_=1, affine=False, vbias=True, projs="QQQV", weights=[(W(0),), (W(1),), (W(2),), (W(3),)],
                             stores=[(qs_d, TERMS_Q), (ks_d, TERMS_K), (qx_d, TERMS_Q)], wo=W(5), resid_bias=True)
        c2 = Part(affine=False, projs="G", weights=[(rw[:, :],)], stores=[], gated=True, capacity=False, resid_bias=False)
        c3 = Part(cross=1, self_=0, affine=False, vbias=False, projs="Q", weights=[(W(0),)],
                             stores=[(qx_d, TERMS_Q)], wo=W(5), resid_bias=True)
        c4 = Part(cross=0, self_=1, affine=True, vbias=False, projs="RRV",
                             weights=[(W(0), W(1)), (W(2), W(3)), (W(4),)],
                             stores=[(qs_d, TERMS_Q), (ks_d, TERMS_K)], wo=W(5), resid_bias=False)
        c5 = Part(affine=True, projs="G", weights=[(rw[:, :],)], stores=[], gated=False, capacity=True, resid_bias=False)
        parts = [("a", c1), ("b", c2), ("c", c3), ("d", c4), ("e", c5)]
        cx_s, ff_s, biased = ctx_sems("cx"), ffn_sems("ff"), sem("biased")
        for n, c in parts:
            c.name = n
            c.items = proj_plan(c)
            c.nth = {"a": 0, "b": 1, "c": 2, "d": 4, "e": 5}[n]
            c.pj = proj_sems(n, c)
            c.attn = n in "acd"
            if c.attn:
                if c.cross:
                    c.cx = cx_s
                    c.turn = n == "c"
                attn_cfg(c, n)
            else:
                c.gt = gate_sems(n)
                c.ff = ff_s
                c.turn = n == "e"
            c.biased = biased

        def copy_in(sp, pairs_):
            for dst, src in pairs_:
                sp.dma_start(dst, src).then_inc(loaded, 16)
                count["in"] = count.get("in", 0) + 16
            sp.wait_ge(loaded, count["in"])

        def part_inputs(n):
            if n == "a":
                return ([(W(i), A["w_a"][i]) for i in range(6)] +
                        [(colv[:, i:i + 1], A["col_a"][i]) for i in range(3)] +
                        [(rowv[:, 0, :], A["bp"]), (rowv[:, 1, :], A["bv"]), (wkv[0:CC + 1, 0, :], A["wk_a"]),
                         (wkv[0:CC + 1, 1, :], A["wv_a"])]), []
            if n == "b":
                return [(rw[:, :], A["rw_b"])], [
                    (w_in, A["wg_b"]), (w_up, A["w1_b"]), (w_out.rearrange("p e k c -> p (e k c)"), A["w2_b"]),
                    (b1s[:, 0], A["bg_b"]), (b1s[:, 1], A["b1_b"]), (b2s[:, :], A["b2_b"])]
            if n == "c":
                return [(W(0), A["w_c"][0]), (W(5), A["w_c"][1]), (colv[:, 0:1], A["col_c"]), (rowv[:, 0, :], A["bo"]),
                        (wkv[0:CC + 1, 0, :], A["wk_c"]), (wkv[0:CC + 1, 1, :], A["wv_c"])], []
            if n == "d":
                return [(W(i), A["w_d"][i]) for i in range(6)] + [(colv[:, 2:3], A["ln1g"]), (colv[:, 3:4], A["ln1b"]),
                                                              (rope[:, :, :], A["rope"])], []
            return [(rw[:, :], A["rw_e"]), (colv[:, 2:3], A["ln2g"]), (colv[:, 3:4], A["ln2b"]),
                    (res, res_d.rearrange("p t c -> p (t c)"))], [
                (w_in, A["w1_e"]), (w_out.rearrange("p e k c -> p (e k c)"), A["w2_e"]), (b1s[:, 0], A["b1_e"]),
                (b2s[:, :], A["b2_e"])]

        block = ctx.enter_context(nc.Block())
        x_dram = A["x"].rearrange("b (q p) c -> p (b q) c", p=P)
        out_dram = out.rearrange("b (q p) c -> p (b q) c", p=P)

        @block.sync
        def _(sp):
            copy_in(sp, [(x3, x_dram)])
            sp.wait_ge(made, 1)
            zero = arenaA[0:3 * H, 0:TOK // 2].bitcast(BF16)
            copy_in(sp, [(d[:, ROWS:ROWSM, :], zero) for d in (qx_d, qs_d)])
            phase_end(sp, "sp")
            for n, c in parts:
                if n == "d":
                    copy_in(sp, [(res_d, x3)])
                    phase_end(sp, "sp")
                    phase_end(sp, "sp")
                small, large = part_inputs(n)
                copy_in(sp, small)
                c.loaded = count["in"]
                if large:
                    copy_in(sp, large)
                proj_sp(sp, c)
                phase_end(sp, "sp")
                if c.attn and c.cross:
                    ctx_sp(sp, c)
                    phase_end(sp, "sp")
                if c.attn:
                    attn_sp(sp, c)
                    phase_end(sp, "sp")
                else:
                    phase_end(sp, "sp")
                    phase_end(sp, "sp")
            sp.dma_start(out_dram, x3).then_inc(loaded, 16)
            sp.wait_ge(loaded, count["in"] + 16)

        @block.gpsimd
        def _(pool):
            k = [0]

            def link(ins):
                k[0] += 1
                ins.then_inc(made, 1)
                pool.wait_ge(made, k[0])

            big = arenaB[:, 0:P]
            link(pool.memset(arenaA[0:3 * H, 0:TOK // 2], 0.0))
            link(pool.memset(eps_col[:, :], EPS))
            link(pool.memset(ones[:, :], 1.0))
            link(pool.memset(ident[:, :], 0.0))
            link(pool.affine_select(out=ident[:, :], in_=ident[:, :], compare_op=ALU.not_equal, fill=1.0, base=0,
                                    pattern=[[-1, P]], channel_multiplier=1))
            link(pool.tensor_copy(ident16[:, :], ident[:, :]))
            link(pool.affine_select(out=upper[:, :], in_=ones[:, :], compare_op=ALU.is_ge, fill=0.0, base=0,
                                    pattern=[[1, P]], channel_multiplier=-1))
            link(pool.memset(big, 0.0))
            link(pool.affine_select(out=big, in_=big, compare_op=ALU.is_ge, fill=MASKED, base=0,
                                    pattern=[[-1, P]], channel_multiplier=1))
            link(pool.tensor_copy(mask_qk[:, :], big))
            link(pool.memset(big, 0.0))
            link(pool.affine_select(out=big, in_=big, compare_op=ALU.is_ge, fill=MASKED, base=0,
                                    pattern=[[1, P]], channel_multiplier=-1))
            link(pool.tensor_copy(mask_kq[:, :], big))
            link(pool.memset(mrow[:, :, :], 0.0))
            for hp in range(2):
                for e in range(2):
                    one, r = big[:, 2 * hp + e:2 * hp + e + 1], 6 * e + hp
                    link(pool.tensor_tensor(one, ident[:, r:r + 1], ident[:, r + 2:r + 3], ALU.add))
                    link(pool.tensor_tensor(one, one, ident[:, r + 4:r + 5], ALU.add))
                    link(pool.tensor_copy(pick[:, hp, e, :], one.to_broadcast([P, P])))
            link(pool.memset(wkv[:, :, :], 0.0))
            for e in range(E):
                link(pool.memset(rank[:, :, e:e + 1], float(E - e)))
            count["made"] = k[0]
            phase_end(pool, "pool")
            for n, c in parts:
                if n == "d":
                    phase_end(pool, "pool")
                    phase_end(pool, "pool")
                if c.attn:
                    attn_pads(pool, c)
                if n == "e" or c.resid_bias:
                    pool.wait_ge(loaded, c.loaded)
                    pool.wait_ge(ln_s.dve, 24 * c.nth + CENTRED[3])
                if n == "e":
                    pool.tensor_tensor(x[:, :], x[:, :], res, ALU.add).then_inc(biased, 1)
                if c.resid_bias:
                    pool.tensor_tensor(x3, x3, rowv[:, 0, :].unsqueeze(1).to_broadcast([P, TILES, C]), ALU.add)\
                        .then_inc(c.biased, 1)
                phase_end(pool, "pool")
                if c.attn and c.cross:
                    phase_end(pool, "pool")
                if c.attn:
                    attn_pool(pool, c)
                    phase_end(pool, "pool")
                else:
                    phase_end(pool, "pool")
                    phase_end(pool, "pool")

        @block.scalar
        def _(act):
            phase_end(act, "act")
            for n, c in parts:
                if n == "d":
                    for j in range(4):
                        ln_act(act, 3, j)
                    phase_end(act, "act")
                    act.activation(x[:, 0:TOK // 2], xn[:, 0:TOK // 2], ACT.Copy)
                    phase_end(act, "act")
                proj_act(act, c)
                phase_end(act, "act")
                if c.attn and c.cross:
                    ctx_act(act, c)
                    phase_end(act, "act")
                if c.attn:
                    attn_act(act, c)
                    phase_end(act, "act")
                else:
                    gates_act(act, c)
                    phase_end(act, "act")
                    ffn_act(act, c)
                    phase_end(act, "act")

        @block.vector
        def _(dve):
            phase_end(dve, "dve")
            for n, c in parts:
                if n == "d":
                    for j in range(4):
                        ln_dve(dve, 3, j)
                    phase_end(dve, "dve")
                    dve.tensor_copy(x[:, TOK // 2:TOK], xn[:, TOK // 2:TOK])
                    phase_end(dve, "dve")
                proj_dve(dve, c)
                phase_end(dve, "dve")
                if c.attn and c.cross:
                    ctx_dve(dve, c)
                    phase_end(dve, "dve")
                if c.attn:
                    attn_dve(dve, c)
                    phase_end(dve, "dve")
                else:
                    gates_dve(dve, c)
                    phase_end(dve, "dve")
                    ffn_dve(dve, c)
                    phase_end(dve, "dve")

        @block.tensor
        def _(pe):
            phase_end(pe, "pe")
            for n, c in parts:
                if n == "d":
                    phase_end(pe, "pe")
                    phase_end(pe, "pe")
                proj_pe(pe, c)
                phase_end(pe, "pe")
                if c.attn and c.cross:
                    ctx_pe(pe, c)
                    phase_end(pe, "pe")
                if c.attn:
                    attn_pe(pe, c)
                    phase_end(pe, "pe")
                else:
                    gates_pe(pe, c)
                    phase_end(pe, "pe")
                    ffn_pe(pe, c)
                    phase_end(pe, "pe")


def lay_out(i):
    import numpy as np
    i = {k: np.asarray(v) for k, v in i.items()}
    col = lambda a: np.ascontiguousarray(a.reshape(C, 1))
    rows = lambda a: np.ascontiguousarray(np.broadcast_to(a, (P, C)))
    withb = lambda w, b: np.concatenate([w, b[None, :]], 0)
    L = "L0_xattn_"
    a = {"x": i["x"], "ctxT": np.ascontiguousarray(i["ctx_512"].transpose(0, 2, 1))}
    a["w_a"] = np.stack([i[L + "Wq"], i[L + "Wk"], i[L + "Wcq"], i[L + "Wv"], i[L + "Wp"], i[L + "Wp"]])
    a["col_a"] = np.stack([col(i[L + n]) for n in ("bq", "bk", "bcq")])
    a["bp"], a["bv"] = rows(i[L + "bp"]), rows(i[L + "bv"])
    a["wk_a"], a["wv_a"] = withb(i[L + "Wck"], i[L + "bck"]), withb(i[L + "Wcv"], i[L + "bcv"])
    L = "L0_ffn_"
    a["rw_b"] = np.ascontiguousarray(i[L + "router_w"].T)
    inw = lambda w: np.ascontiguousarray(w.transpose(2, 0, 1).reshape(C, E * F))
    a["wg_b"], a["w1_b"] = inw(i[L + "wg_w"]), inw(i[L + "w1_w"])
    a["w2_b"] = np.ascontiguousarray(i[L + "w2_w"].reshape(E, C, FC, P).transpose(3, 0, 2, 1).reshape(P, E * FC * C))
    bias = lambda b: np.ascontiguousarray(b.reshape(E, FC, P).transpose(2, 0, 1))
    a["bg_b"], a["b1_b"], a["b2_b"] = bias(i[L + "wg_b"]), bias(i[L + "w1_b"]), i[L + "w2_b"]
    L = "L1_xattn_"
    a["w_c"] = np.stack([i[L + "Wq"], i[L + "Wo"]])
    a["col_c"], a["bo"] = col(i[L + "bq"]), rows(i[L + "bo"])
    a["wk_c"], a["wv_c"] = withb(i[L + "Wk"], i[L + "bk"]), withb(i[L + "Wv"], i[L + "bv"])
    L = "L1_ffn_"
    w = i[L + "Wqkv"].reshape(C, H, 3, D)
    wq, wk, wv = (np.ascontiguousarray(w[:, :, n, :]).reshape(C, C) for n in range(3))
    half = D // 2
    turn = np.array([h * D + (d + half) % D for h in range(H) for d in range(D)])
    a["w_d"] = np.stack([wq, wq[:, turn], wk, wk[:, turn], wv, i[L + "Wproj"]])
    inv = (1.0 / 10000.0 ** (np.arange(0, D, 2, dtype=np.float32) / D)).astype(np.float32)
    ang = np.arange(T, dtype=np.float32)[:, None] * inv
    cos, sin = np.cos(ang).T, np.sin(ang).T
    a["rope"] = np.stack([np.tile(np.concatenate([cos, cos]), (H, 1)),
                          np.tile(np.concatenate([-sin, sin]), (H, 1))], 1).astype(np.float32)
    a["ln1g"], a["ln1b"] = col(i[L + "ln1_g"]), col(i[L + "ln1_b"])
    a["ln2g"], a["ln2b"] = col(i[L + "ln2_g"]), col(i[L + "ln2_b"])
    a["rw_e"] = i[L + "Wgate"]
    a["w1_e"] = np.ascontiguousarray(i[L + "W1"].transpose(1, 0, 2).reshape(C, E * F))
    a["w2_e"] = np.ascontiguousarray(i[L + "W2"].reshape(E, FC, P, C).transpose(2, 0, 1, 3).reshape(P, E * FC * C))
    a["b1_e"], a["b2_e"] = bias(i[L + "b1"]), i[L + "b2"]
    return {k: np.ascontiguousarray(v) for k, v in a.items()}


def kernel(**inputs):
    import concourse.bacc as bacc
    from concourse.bass_utils import run_bass_kernel_spmd

    arrays = lay_out(inputs)
    nc = bacc.Bacc("TRN2", target_bir_lowering=False, num_devices=1)
    aps = {k: nc.dram_tensor(f"in_{k}", v.shape, mybir.dt.from_np(v.dtype), kind="ExternalInput").ap()
           for k, v in arrays.items()}
    out = nc.dram_tensor("out_x", (B, T, C), F32, kind="ExternalOutput").ap()
    build(nc, aps, out)
    r = run_bass_kernel_spmd(nc, [{f"in_{k}": v for k, v in arrays.items()}], core_ids=[0])
    return r.results[0]["out_x"]
```
